# Optimizing a Trainium2 kernel written in Bass

```python
import numpy as np
import jax
import jax.numpy as jnp

def _softmax(x, axis=-1):
    return jax.nn.softmax(x, axis=axis)

def _gelu(x):
    return jax.nn.gelu(x, approximate=True)

def _silu(x):
    return jax.nn.silu(x)

def _sigmoid(x):
    return jax.nn.sigmoid(x)

def _layernorm(x, axis=-1, eps=1e-05):
    m = jnp.mean(x, axis=axis, keepdims=True)
    v = jnp.var(x, axis=axis, keepdims=True)
    return (x - m) / jnp.sqrt(v + eps)

def _scatter_add(tgt, idx, src, axis=0):
    return tgt.at[idx].add(src)

def _segment_sum(src, seg, n):
    return jax.ops.segment_sum(src, seg, n)
kernel_name = 'mk_flamingo_gated_d1_seqx_r4_e28f19'

def setup_inputs(seed: int=0):
    np.random.seed(seed)
    _w = jnp.asarray

    def _rec_inputs():
        import jax
        import jax.numpy as jnp
        _rk = jax.random.key(seed)
        x = -0.000125 + 0.9999 * jax.random.normal(jax.random.fold_in(_rk, 1), (4, 512, 512), jnp.float32)
        _lenS = 512 - jax.random.randint(jax.random.fold_in(_rk, 7), (4,), 0, max(1, 512 // 4) + 1, jnp.int32)
        _lenS2 = 512 - jax.random.randint(jax.random.fold_in(_rk, 8), (4,), 0, max(1, 512 // 4) + 1, jnp.int32)
        itok_BxS_13_99985 = jax.random.randint(jax.random.fold_in(_rk, 11), (4, 512), 13, 99986, jnp.int32)
        _ctx_2048P = jax.random.normal(jax.random.fold_in(_rk, 12), (4, 16, 512), jnp.float32)
        _ctx_2048c = jax.random.dirichlet(jax.random.fold_in(_rk, 512), 0.3 * jnp.ones((16,), jnp.float32), (4, 512))
        _ctx_2048t = jnp.einsum('bsk,bkd->bsd', _ctx_2048c, _ctx_2048P)
        _ctx_2048t = _ctx_2048t * jax.lax.rsqrt(jnp.mean(jnp.square(_ctx_2048t)) + 1e-12) * 0.953939
        ctx_2048 = 6.82029e-06 + 0.0200006 * (_ctx_2048t + 0.3 * jax.random.normal(jax.random.fold_in(_rk, 612), (4, 512, 512), jnp.float32))
        _g = jax.random.normal(jax.random.fold_in(_rk, 9001), (2, 1), jnp.float32)
        _g = jnp.sign(_g) * jnp.maximum(jnp.abs(_g), 1.0) + (_g == 0) * 1.0
        g_xattn = _g[0]
        g_ffn = _g[1]
        return (x, itok_BxS_13_99985, ctx_2048, g_xattn, g_ffn)
    x, itok_BxS_13_99985, ctx_2048, g_xattn, g_ffn = _rec_inputs()

    def _L0_xattn_setup():
        import jax, jax.numpy as jnp
        import numpy as np
        B, S, D = (4, 1024, 512)
        E = 4
        F = 2048 // E
        VOCAB = 25000
        key = jax.random.key(seed)
        k1, k2, k3, k4, k5 = jax.random.split(key, 5)
        hidden_states = jax.random.normal(k1, (B, S, D), dtype=jnp.float32)
        token_ids = jax.random.randint(k2, (B, S), 0, VOCAB, dtype=jnp.int64)
        Wg = jax.random.normal(k3, (E, F, D), dtype=jnp.float32) * 0.02
        Wu = jax.random.normal(k4, (E, F, D), dtype=jnp.float32) * 0.02
        Wd = jax.random.normal(k5, (E, D, F), dtype=jnp.float32) * 0.02
        return {'hidden_states': hidden_states, 'token_ids': token_ids, 'Wg': Wg, 'Wu': Wu, 'Wd': Wd}
    _L0_xattn_all = _L0_xattn_setup()
    _L0_xattn_in = {k: v for k, v in _L0_xattn_all.items() if k in ()}
    del _L0_xattn_all

    def _L0_ffn_setup():
        import jax, jax.numpy as jnp
        import numpy as np
        B, S, H, I = (1, 64, 512, 1536)

        def _quantized_matmul(x, w, scale):
            wq = w.astype(jnp.float8_e4m3fn).astype(x.dtype)
            y = jnp.einsum('bsi,io->bso', x, wq)
            return y * scale
        key = jax.random.key(seed)
        ks = jax.random.split(key, 7)
        return {'x': jax.random.normal(ks[0], (B, S, H), dtype=jnp.float32), 'gate_w': jax.random.normal(ks[1], (H, I), dtype=jnp.float32) * 0.02, 'up_w': jax.random.normal(ks[2], (H, I), dtype=jnp.float32) * 0.02, 'down_w': jax.random.normal(ks[3], (I, H), dtype=jnp.float32) * 0.02, 'gate_scale': jax.random.uniform(ks[4], (I,), dtype=jnp.float32, minval=0.5, maxval=1.5), 'up_scale': jax.random.uniform(ks[5], (I,), dtype=jnp.float32, minval=0.5, maxval=1.5), 'down_scale': jax.random.uniform(ks[6], (H,), dtype=jnp.float32, minval=0.5, maxval=1.5)}
    _L0_ffn_all = _L0_ffn_setup()
    _L0_ffn_in = {k: v for k, v in _L0_ffn_all.items() if k in ('gate_w', 'up_w', 'down_w', 'gate_scale', 'up_scale', 'down_scale')}
    del _L0_ffn_all
    return {'x': x, 'itok_BxS_13_99985': itok_BxS_13_99985, 'ctx_2048': ctx_2048, 'g_xattn': g_xattn, 'g_ffn': g_ffn, 'L0_ffn_gate_w': _L0_ffn_in['gate_w'], 'L0_ffn_up_w': _L0_ffn_in['up_w'], 'L0_ffn_down_w': _L0_ffn_in['down_w'], 'L0_ffn_gate_scale': _L0_ffn_in['gate_scale'], 'L0_ffn_up_scale': _L0_ffn_in['up_scale'], 'L0_ffn_down_scale': _L0_ffn_in['down_scale']}

def reference(x, itok_BxS_13_99985, ctx_2048, g_xattn, g_ffn, L0_ffn_gate_w, L0_ffn_up_w, L0_ffn_down_w, L0_ffn_gate_scale, L0_ffn_up_scale, L0_ffn_down_scale):
    import jax
    import jax.numpy as jnp

    def _L0_xattn_ref(hidden_states, token_ids, Wg, Wu, Wd):
        import jax, jax.numpy as jnp
        import numpy as np
        B, S, D = (4, 1024, 512)
        E = 4
        F = 2048 // E
        VOCAB = 25000
        tokens_per_expert = VOCAB // E
        tid = jnp.clip(token_ids, 0, VOCAB - 1)
        expert_ids = jnp.minimum(tid // tokens_per_expert, E - 1)
        out = jnp.zeros_like(hidden_states)
        for e in range(E):
            g = jax.nn.silu(jnp.einsum('bsd,fd->bsf', hidden_states, Wg[e]))
            u = jnp.einsum('bsd,fd->bsf', hidden_states, Wu[e])
            y = jnp.einsum('bsf,df->bsd', g * u, Wd[e])
            out = jnp.where((expert_ids == e)[..., None], y, out)
        return out

    def _L0_ffn_ref(x, gate_w, up_w, down_w, gate_scale, up_scale, down_scale):
        import jax, jax.numpy as jnp
        import numpy as np
        B, S, H, I = (1, 64, 512, 1536)

        def _quantized_matmul(x, w, scale):
            wq = w.astype(jnp.float8_e4m3fn).astype(x.dtype)
            y = jnp.einsum('bsi,io->bso', x, wq)
            return y * scale
        gate = jax.nn.silu(_quantized_matmul(x, gate_w, gate_scale))
        up = _quantized_matmul(x, up_w, up_scale)
        fuse = gate * up
        return _quantized_matmul(fuse, down_w, down_scale)
    x = x + jnp.tanh(g_xattn[0]) * _L0_xattn_ref(_layernorm(x, axis=-1), itok_BxS_13_99985, ctx_2048, ctx_2048, ctx_2048)
    x = x + jnp.tanh(g_ffn[0]) * _L0_ffn_ref(_layernorm(x, axis=-1), L0_ffn_gate_w, L0_ffn_up_w, L0_ffn_down_w, L0_ffn_gate_scale, L0_ffn_up_scale, L0_ffn_down_scale)
    return x

_drawn_inputs = setup_inputs


def setup_inputs(seed=0):
    import zlib

    import numpy as np

    out = dict(_drawn_inputs(seed))
    spreads = {}
    factors = {}
    for name, (base, spread) in spreads.items():
        noise = np.random.default_rng([zlib.crc32(name.encode()), seed]).standard_normal(out[name].shape)
        drawn = base * np.exp(spread * noise) if base else spread * noise
        out[name] = jnp.asarray(drawn.astype(out[name].dtype))
    for name, factor in factors.items():
        out[name] = (out[name] * factor).astype(out[name].dtype)
    return out
```

```python
from contextlib import ExitStack

import concourse.bass as bass
from concourse import mybir

F32, F16, BF16, I32 = mybir.dt.float32, mybir.dt.float16, mybir.dt.bfloat16, mybir.dt.int32
ALU = mybir.AluOpType
ACT = mybir.ActivationFunctionType
AX = mybir.AxisListType
RMAX = bass.bass_isa.ReduceOp.max
ds = bass.ds

P = 128
LN_EPS = 1e-5
VOCAB, EXPERTS = 25000, 4
PER_EXPERT = VOCAB // EXPERTS
X_SCALE = 2.0 ** 11
POW2_MASK = 0x7F800000
FP8_STEP = 2.0 ** 20
FP8_FLOOR = FP8_STEP * 2.0 ** -6 * (1 + 2.0 ** -19)


def build(nc, x, token_ids, ctx, g_xattn, g_ffn, gate_w, up_w, down_w, gate_scale, up_scale, down_scale, out):
    B, S, D = x.shape
    TOK = B * S
    TILES = TOK // P
    E = ctx.shape[0]
    KC = D // P
    INNER = gate_w.shape[1]
    IC = INNER // P
    STEPS = TILES + E - 1
    GROUPS = TOK // 512
    TPG = TILES // GROUPS
    THIRDS = INNER // 512
    PAIRS = 3 * IC // 2
    GU_PAIRS = 2 * IC // 2
    LN2_LAG = 5
    assert E == EXPERTS and KC == 4 and D == 512 and PAIRS == STEPS - 1

    x_rows = x.rearrange("b s d -> (b s) d")
    out_rows = out.rearrange("b s d -> (b s) d")
    ids_v = token_ids.rearrange("b s -> (b s)").rearrange("(p c) -> p c", c=TILES)
    ctx_v = ctx.rearrange("e (r p) d -> e p r d", p=P)
    gate_v = gate_w.rearrange("(k p) n -> p k n", p=P)
    up_v = up_w.rearrange("(k p) n -> p k n", p=P)
    down_v = down_w.rearrange("(k p) n -> p k n", p=P)

    with ExitStack() as stack:
        def sb(name, shape, dt):
            return stack.enter_context(nc.sbuf_tensor(name, shape, dt))

        def sem(name):
            return stack.enter_context(nc.semaphore(name))

        xs = sb("xs", [P, TILES, D], F32)
        Mh = sb("Mh", [P, E * KC * 512], F16)
        Ml = sb("Ml", [P, E * KC * 512], F16)
        X2 = sb("X2", [P, GROUPS, 2, KC, TPG, P], F16)
        W8 = sb("W8", [P, 3 * IC, 512], BF16)
        cs = sb("cs", [P, 2, KC, D], F32)
        ws = sb("ws", [P, 2, 2, 512], F32)
        w_big = sb("w_big", [P, 2, 2, 512], F32)
        w_sum = sb("w_sum", [P, 2, 512], F32)
        qd = sb("qd", [P, 2, 512], BF16)
        sq = sb("sq", [P, 2, 512], BF16)
        junk = sb("junk", [P, 512], F32)
        xn = sb("xn", [P, D], F32)
        x2n = sb("x2n", [P, D], F32)
        xTh = sb("xTh", [P, KC * P], F16)
        xTl = sb("xTl", [P, KC * P], F16)
        hTh = sb("hTh", [P, KC * P], F16)
        hTl = sb("hTl", [P, KC * P], F16)
        silu_z = sb("silu_z", [P, 512], F32)
        h = sb("h", [P, 512], F32)
        sg = cs[:, 0, 0:2, :]
        fuse = cs[:, 0, 2:4, :]
        fh = cs[:, 1, 0:1, :].rearrange("p a n -> p (a n)").bitcast(F16).rearrange("p (b n) -> p b n", b=2)
        fl = cs[:, 1, 1:2, :].rearrange("p a n -> p (a n)").bitcast(F16).rearrange("p (b n) -> p b n", b=2)
        ident = sb("ident", [P, P], F32)
        zero = sb("zero", [P, P], F32)
        below = sb("below", [P, P], BF16)
        ones = sb("ones", [P, P], BF16)
        iota_q = sb("iota_q", [P, P], F32)
        tok_no = sb("tok_no", [P, TILES], F32)
        step128 = sb("step128", [P, STEPS], F32)
        step_pos = sb("step_pos", [P, STEPS], F32)
        ones64 = sb("ones64", [P, E * TILES], F32)
        ln_eps = sb("ln_eps", [P, 2], F32)
        x_scale = sb("x_scale", [P, 2], F32)
        x_neg = sb("x_neg", [P, 2], F32)
        mhalf = sb("mhalf", [P, IC], F32)
        ids = sb("ids", [P, TILES], I32)
        idf = sb("idf", [P, TILES], F32)
        cge = sb("cge", [P, E + 1, TILES], F32)
        onehot = sb("onehot", [P, E * TILES], BF16)
        total = sb("total", [P, E * TILES], F32)
        incl = sb("incl", [P, E * TILES], F32)
        base = sb("base", [P, E * TILES], F32)
        rank_e = sb("rank_e", [P, E * TILES], F32)
        rank_m = sb("rank_m", [P, E * TILES], F32)
        rank = sb("rank", [P, TILES], F32)
        rank_i = sb("rank_i", [P, TILES], I32)
        row_i = sb("row_i", [P, TILES], I32)
        tile_i = sb("tile_i", [P, TILES], I32)
        row_f = sb("row_f", [P, TILES], F32)
        tile_f = sb("tile_f", [P, TILES], F32)
        row_hot = sb("row_hot", [P, TILES, P], F16)
        tile_eq = sb("tile_eq", [P, TILES, TILES], F32)
        tile_tok = sb("tile_tok", [P, TILES, TILES], F16)
        order = sb("order", [P, TILES], I32)
        bound = sb("bound", [P, E - 1], F32)
        past = sb("past", [P, E - 1, STEPS], F32)
        past2 = sb("past2", [P, STEPS], F32)
        e_of = sb("e_of", [P, STEPS], F32)
        pos = sb("pos", [P, STEPS], F32)
        cnt = sb("cnt", [P, E - 1, STEPS], F32)
        cnt2 = sb("cnt2", [P, STEPS], F32)
        cnt3 = sb("cnt3", [P, STEPS], F32)
        mask = sb("mask", [P, STEPS], F32)
        walk_f = sb("walk_f", [P, STEPS], F32)
        walk = sb("walk", [P, 2, STEPS], I32)
        gx = sb("gx", [P, 1], F32)
        gf = sb("gf", [P, 1], F32)
        tgx = sb("tgx", [P, 1], F32)
        tgf = sb("tgf", [P, 1], F32)
        tgx24 = sb("tgx24", [P, 1], F32)
        gs_rows = sb("gs_rows", [IC, P], F32)
        us_rows = sb("us_rows", [IC, P], F32)
        gs = sb("gs", [P, IC], F32)
        us = sb("us", [P, IC], F32)
        dsc = sb("dsc", [P, D], F32)
        dsb = sb("dsb", [P, D], F32)
        row_ssq = sb("row_ssq", [P, E, KC], F32)
        row_max = sb("row_max", [P, E], F32)
        all_max = sb("all_max", [P, E], F32)
        n2 = sb("n2", [P, E], F32)
        n_inv = sb("n_inv", [P, E], F32)
        n_top = sb("n_top", [P, E], F32)
        m_scale = sb("m_scale", [P, E], F32)
        m_inv = sb("m_inv", [P, E], F32)
        m_inv2 = sb("m_inv2", [P, E], F32)
        z_scale = sb("z_scale", [P, E], F32)
        h_scale = sb("h_scale", [P, E], F32)
        y_scale = sb("y_scale", [P, E], F32)
        row_scale = sb("row_scale", [P, STEPS], F32)
        stats = sb("stats", [P, 2, 6], F32)
        mv = sb("mv", [P, 2, 2], F32)
        var_eps = sb("var_eps", [P, 2], F32)
        rstd = sb("rstd", [P, 2], F32)
        ln_mul = sb("ln_mul", [P, 2], F32)
        ln_neg = sb("ln_neg", [P, 2], F32)
        ln_add = sb("ln_add", [P, 2], F32)
        col_ssq = sb("col_ssq", [P, 2, IC], F32)
        gu = sb("gu", [P, IC], F32)
        gu2 = sb("gu2", [P, IC], F32)
        nn = sb("nn", [P, IC], F32)
        b2 = sb("b2", [P, IC], F32)
        b2c = sb("b2c", [P, IC], F32)
        b_inv = sb("b_inv", [P, IC], F32)
        f_top = sb("f_top", [P, IC], F32)
        f_scale = sb("f_scale", [P, IC], F32)
        f_inv = sb("f_inv", [P, IC], F32)
        gate_mul = sb("gate_mul", [P, IC], F32)
        up_mul0 = sb("up_mul0", [P, IC], F32)
        up_mul = sb("up_mul", [P, IC], F32)

        bank = [stack.enter_context(nc.psum_tensor(f"bank{i}", [P, 512], F32)) for i in range(8)]
        Z, HT, XT, Y, X2T, SMALL = bank[0], bank[1], bank[2], bank[3], bank[4], bank[6]
        MT = [bank[5], bank[7]]
        ACC = [bank[0], bank[1], bank[2], bank[3]]
        GATE = [bank[5], bank[7]]
        UP = [bank[6], bank[4]]

        consts = sem("consts")
        ids_in = sem("ids_in")
        params_in = sem("params_in")
        ctx_in = [sem("ctx_in0"), sem("ctx_in1")]
        w_in = [sem("w_in0"), sem("w_in1")]
        sort_v = sem("sort_v")
        onehot_done = sem("onehot_done")
        counts_done = sem("counts_done")
        place_done = sem("place_done")
        row_hot_done = sem("row_hot_done")
        tile_eq_done = sem("tile_eq_done")
        tile_tok_done = sem("tile_tok_done")
        order_mm = sem("order_mm")
        order_done = sem("order_done")
        gathered = [sem("gathered0"), sem("gathered1"), sem("gathered2")]
        walk_done = sem("walk_done")
        scales_T = sem("scales_T")
        scales_done = sem("scales_done")
        tanh_done = sem("tanh_done")
        gates_done = sem("gates_done")
        ssq_done = sem("ssq_done")
        rmax_done = sem("rmax_done")
        pool_m = sem("pool_m")
        ninv_done = sem("ninv_done")
        mchain = sem("mchain")
        mscale_done = sem("mscale_done")
        mT_done = sem("mT_done")
        mhi_done = sem("mhi_done")
        mlo_done = sem("mlo_done")
        stats_done = sem("stats_done")
        mv_done = sem("mv_done")
        ln_chain = sem("ln_chain")
        ln_done = sem("ln_done")
        rows_done = sem("rows_done")
        xn_done = sem("xn_done")
        xT_done = sem("xT_done")
        xhi_done = sem("xhi_done")
        xlo_done = sem("xlo_done")
        z_done = sem("z_done")
        silu_done = sem("silu_done")
        h_done = sem("h_done")
        hT_done = sem("hT_done")
        hhi_done = sem("hhi_done")
        hlo_done = sem("hlo_done")
        y_done = sem("y_done")
        x1_done = sem("x1_done")
        x2n_done = sem("x2n_done")
        x2T_done = sem("x2T_done")
        x2hi_done = sem("x2hi_done")
        x2lo_done = sem("x2lo_done")
        abs_done = sem("abs_done")
        big_done = sem("big_done")
        sum_done = sem("sum_done")
        q_done = sem("q_done")
        q_used = sem("q_used")
        norm_done = sem("norm_done")
        fchain = sem("fchain")
        b2_done = sem("b2_done")
        pool_f = sem("pool_f")
        binv_done = sem("binv_done")
        fscale_done = sem("fscale_done")
        gate_done = sem("gate_done")
        up_done = sem("up_done")
        sg_done = sem("sg_done")
        fuse_done = sem("fuse_done")
        fh_done = sem("fh_done")
        fl_done = sem("fl_done")
        down_done = sem("down_done")
        acc_done = sem("acc_done")
        acc_free = sem("acc_free")
        added = sem("added")
        stored = sem("stored")

        N_CONSTS = 15

        def slab_tile(g, t):
            v = X2[:, g, :, :, :, :] if isinstance(g, int) else X2[:, ds(g, 1), :, :, :, :]
            pat = "p a k t i -> p (a k t i)" if isinstance(g, int) else "p g a k t i -> p (g a k t i)"
            return v.rearrange(pat).bitcast(F32)[:, t * D:(t + 1) * D]

        def x2_part(tile, part):
            if isinstance(tile, int):
                return X2[:, tile // TPG, part, :, tile % TPG, :]
            return X2[:, ds(tile >> 2, 1), part, :, ds(tile & 3, 1), :].rearrange("p a k b i -> p (a k b) i")

        def x2_group(g, part, k):
            if isinstance(g, int):
                return X2[:, g, part, k, :, :].rearrange("p t i -> p (t i)")
            return X2[:, ds(g, 1), part, k, :, :].rearrange("p g t i -> p (g t i)")

        block = stack.enter_context(nc.Block())

        @block.sync
        def _(sp):
            sp.dma_start(ids[:], ids_v).then_inc(ids_in, 16)
            sp.dma_start(cs[:, 0], ctx_v[E - 1]).then_inc(ctx_in[0], 16)
            sp.dma_start(gx[:], g_xattn.partition_broadcast(P)).then_inc(params_in, 16)
            sp.dma_start(gf[:], g_ffn.partition_broadcast(P)).then_inc(params_in, 16)
            sp.dma_start(gs_rows[:], gate_scale.rearrange("(c p) -> c p", p=P)).then_inc(params_in, 16)
            sp.dma_start(us_rows[:], up_scale.rearrange("(c p) -> c p", p=P)).then_inc(params_in, 16)
            sp.dma_start(dsc[:], down_scale.partition_broadcast(P)).then_inc(params_in, 16)
            sp.dma_start(cs[:, 1], ctx_v[E - 2]).then_inc(ctx_in[1], 16)

            def load_pair(n):
                if n >= 2:
                    sp.wait_ge(sum_done, n - 1)
                if n < GU_PAIRS:
                    w, m = (gate_v, n) if n < GU_PAIRS // 2 else (up_v, n - GU_PAIRS // 2)
                    a, k = m // 2, 2 * (m % 2)
                    src = w[:, k:k + 2, a * 512:(a + 1) * 512]
                else:
                    d = 2 * (n - GU_PAIRS)
                    src = down_v[:, d:d + 2, :]
                sp.dma_start(ws[:, n % 2], src).then_inc(w_in[n % 2], 16)

            load_pair(0)
            load_pair(1)
            for e in range(2, E):
                sp.wait_ge(mT_done, KC * (e - 1))
                sp.wait_ge(ssq_done, KC * (e - 1))
                sp.dma_start(cs[:, e % 2], ctx_v[E - 1 - e]).then_inc(ctx_in[e % 2], 16)
            for n in range(2, PAIRS):
                load_pair(n)

        @block.gpsimd
        def _(pool):
            g = nc.gpsimd
            g.memset(zero[:], 0.0).then_inc(consts, 1)
            g.memset(ones[:], 1.0).then_inc(consts, 1)
            g.memset(mhalf[:], -0.5).then_inc(consts, 1)
            g.memset(ones64[:], 1.0).then_inc(consts, 1)
            g.memset(ln_eps[:], LN_EPS).then_inc(consts, 1)
            g.memset(x_scale[:], X_SCALE).then_inc(consts, 1)
            g.memset(x_neg[:], -X_SCALE).then_inc(consts, 1)
            g.iota(iota_q[:], pattern=[[1, P]], base=0, channel_multiplier=0,
                   allow_small_or_imprecise_dtypes=True).then_inc(consts, 1)
            g.iota(tok_no[:], pattern=[[1, TILES]], base=0, channel_multiplier=TILES,
                   allow_small_or_imprecise_dtypes=True).then_inc(consts, 1)
            g.iota(step128[:], pattern=[[P, STEPS]], base=0, channel_multiplier=0,
                   allow_small_or_imprecise_dtypes=True).then_inc(consts, 1)
            g.iota(step_pos[:], pattern=[[P, STEPS]], base=0, channel_multiplier=1,
                   allow_small_or_imprecise_dtypes=True).then_inc(consts, 1)
            g.memset(cge[:, 0], 0.0).then_inc(consts, 1)
            g.memset(cge[:, E], 1.0).then_inc(consts, 1)
            pool.wait_ge(consts, N_CONSTS - 2)
            g.affine_select(out=ident[:], in_=zero[:], compare_op=ALU.not_equal, fill=1.0, base=0,
                            pattern=[[-1, P]], channel_multiplier=1).then_inc(consts, 1)
            g.affine_select(out=below[:], in_=ones[:], compare_op=ALU.is_gt, fill=0.0, base=0,
                            pattern=[[1, P]], channel_multiplier=-1).then_inc(consts, 1)

            pool.wait_ge(tile_eq_done, 1)
            g.tensor_tensor(tile_tok[:], tile_eq[:], tok_no[:].unsqueeze(2).to_broadcast([P, TILES, TILES]),
                            ALU.mult).then_inc(tile_tok_done, 1)

            pool.wait_ge(order_done, 1)

            def gather(t, done):
                g.indirect_dma_start(out=xs[:, t, :], out_offset=None, in_=x_rows[:],
                                     in_offset=bass.IndirectOffsetOnAxis(ap=order[:, t:t + 1], axis=0)
                                     ).then_inc(done, 16)

            for t in range(4):
                gather(t, gathered[min(t, 1)])

            def expert_norm(e):
                pool.wait_ge(rmax_done, e + 1)
                g.partition_all_reduce(all_max[:, e:e + 1], row_max[:, e:e + 1], P, RMAX).then_inc(pool_m, 1)
                pool.wait_ge(pool_m, 3 * e + 1)
                g.tensor_scalar(n2[:, e:e + 1], all_max[:, e:e + 1], 2.0 ** -40, None, ALU.max).then_inc(pool_m, 1)
                pool.wait_ge(pool_m, 3 * e + 2)
                g.tensor_tensor(n_inv[:, e:e + 1], n2[:, e:e + 1], mhalf[:, 0:1], ALU.pow).then_inc(pool_m, 1)
                pool.wait_ge(pool_m, 3 * e + 3)
                g.tensor_scalar(n_top[:, e:e + 1], n_inv[:, e:e + 1], 2.0 ** 15, None,
                                ALU.mult).then_inc(ninv_done, 1)

            def ln_scalars(n, lo, hi, reads):
                pool.wait_ge(mv_done, n + 1)
                for s_, v in reads:
                    pool.wait_ge(s_, v)
                g.tensor_tensor(var_eps[:, lo:hi], mv[:, lo:hi, 1], ln_eps[:, lo:hi], ALU.add).then_inc(ln_chain, 1)
                pool.wait_ge(ln_chain, 4 * n + 1)
                g.tensor_tensor(rstd[:, lo:hi], var_eps[:, lo:hi], mhalf[:, lo:hi], ALU.pow).then_inc(ln_chain, 1)
                pool.wait_ge(ln_chain, 4 * n + 2)
                g.tensor_tensor(ln_mul[:, lo:hi], rstd[:, lo:hi], x_scale[:, lo:hi], ALU.mult).then_inc(ln_chain, 1)
                g.tensor_tensor(ln_neg[:, lo:hi], rstd[:, lo:hi], x_neg[:, lo:hi], ALU.mult).then_inc(ln_chain, 1)
                pool.wait_ge(ln_chain, 4 * n + 4)
                g.tensor_tensor(ln_add[:, lo:hi], mv[:, lo:hi, 0], ln_neg[:, lo:hi], ALU.mult).then_inc(ln_done, 1)

            expert_norm(0)
            ln_scalars(0, 0, 1, [])

            def step(s, lo):
                both = lo >= LN2_LAG
                if lo < STEPS - 1:
                    reads = [(xn_done, s + 1)]
                    if lo > LN2_LAG:
                        reads.append((x2n_done, s - LN2_LAG))
                    ln_scalars(s + 1, 0, 2 if both else 1, reads)
                if lo == 0:
                    pool.wait_ge(walk_done, 2)
                if lo < E:
                    pool.wait_ge(mscale_done, min(lo, E - 1) + 1)
                e = g.value_load(walk[0:1, 0, ds(s, 1)], min_val=0, max_val=E - 1)
                g.tensor_tensor(row_scale[:, ds(s, 1)], mask[:, ds(s, 1)], y_scale[:, ds(e, 1)],
                                ALU.mult).then_inc(rows_done, 1)
                if lo + 1 < E:
                    expert_norm(lo + 1)
                if lo < 3:
                    for t in range(4 + 4 * lo, 8 + 4 * lo):
                        gather(t, gathered[2])
                if lo < PAIRS:
                    pool.wait_ge(big_done, s + 1)
                    g.tensor_tensor(w_sum[:], ws[:, lo % 2], w_big[:, lo % 2], ALU.add).then_inc(sum_done, 1)
                    pool.wait_ge(sum_done, s + 1)
                    if lo < GU_PAIRS:
                        dst = W8[:, ds(2 * s, 2), :]
                    else:
                        dst = qd[:]
                        pool.wait_ge(q_used, s)
                    g.tensor_tensor(dst, w_sum[:], w_big[:, lo % 2], ALU.subtract).then_inc(q_done, 1)

            def ffn_norm():
                pool.wait_ge(b2_done, 1)
                g.tensor_tensor(b_inv[:], b2c[:], mhalf[:], ALU.pow).then_inc(pool_f, 1)
                pool.wait_ge(pool_f, 1)
                g.tensor_scalar(f_top[:], b_inv[:], 2.0 ** 15 / 512, None, ALU.mult).then_inc(binv_done, 1)

            for s in range(6):
                step(s, s)
            with pool.Fori(3, 6) as half:
                step(2 * half, 6)
                step(2 * half + 1, 7)
            ffn_norm()
            with pool.Fori(6, 9) as half:
                step(2 * half, 12)
                step(2 * half + 1, 13)
            for i, t in enumerate(range(STEPS - 1 - LN2_LAG, TILES)):
                ln_scalars(STEPS + i, 1, 2, [(x2n_done, t)])
                if i == 0:
                    e = g.value_load(walk[0:1, 0, STEPS - 1:STEPS], min_val=0, max_val=E - 1)
                    g.tensor_tensor(row_scale[:, STEPS - 1:STEPS], mask[:, STEPS - 1:STEPS],
                                    y_scale[:, ds(e, 1)], ALU.mult).then_inc(rows_done, 1)

            for t in range(TILES):
                pool.wait_ge(acc_free, TPG + t + 1)
                g.tensor_tensor(xs[:, t, :], xs[:, t, :], slab_tile(t // TPG, t % TPG), ALU.add).then_inc(added, 1)
                pool.wait_ge(added, t + 1)
                g.indirect_dma_start(out=out_rows[:], out_offset=bass.IndirectOffsetOnAxis(
                    ap=order[:, t:t + 1], axis=0), in_=xs[:, t, :], in_offset=None).then_inc(stored, 16)
            pool.wait_ge(stored, 16 * TILES)

        @block.scalar
        def _(act):
            a = nc.scalar
            act.wait_ge(params_in, 80)
            a.activation(tgx[:], gx[:], ACT.Tanh).then_inc(tanh_done, 1)
            a.activation(tgf[:], gf[:], ACT.Tanh).then_inc(tanh_done, 1)

            def squares(e):
                act.wait_ge(ctx_in[e % 2], 16 * (e // 2 + 1))
                for r in range(KC):
                    if e or r:
                        act.wait_ge(ssq_done, KC * e + r)
                    a.activation(junk[:], cs[:, e % 2, r, :], ACT.Square,
                                 accum_out=row_ssq[:, e, r:r + 1]).then_inc(ssq_done, 1)

            def expert_high(e, chunks):
                act.wait_ge(mscale_done, e + 1)
                for k in chunks:
                    act.wait_ge(mT_done, KC * e + k + 1)
                    a.activation(Mh[:, (e * KC + k) * 512:(e * KC + k + 1) * 512], MT[k % 2][:], ACT.Identity,
                                 scale=m_scale[:, e:e + 1]).then_inc(mhi_done, 1)

            def normalise(tile):
                a.activation(xn[:], xs[:, ds(tile, 1), :].rearrange("p a d -> p (a d)"), ACT.Identity,
                             scale=ln_mul[:, 0:1], bias=ln_add[:, 0:1]).then_inc(xn_done, 1)

            def x_high(s):
                act.wait_ge(xT_done, s + 1)
                a.activation(xTh[:], XT[:], ACT.Copy).then_inc(xhi_done, 1)

            def normalise2(tile, rounds):
                act.wait_ge(ln_done, rounds)
                src = xs[:, tile, :] if isinstance(tile, int) else xs[:, ds(tile, 1), :].rearrange("p a d -> p (a d)")
                if not (isinstance(tile, int) and tile == 0):
                    act.wait_ge(x2T_done, tile)
                a.activation(x2n[:], src, ACT.Identity, scale=ln_mul[:, 1:2],
                             bias=ln_add[:, 1:2]).then_inc(x2n_done, 1)

            def x2_high(tile, src):
                act.wait_ge(x2T_done, tile + 1)
                a.activation(x2_part(tile, 0), src[:].rearrange("p (k i) -> p k i", k=KC),
                             ACT.Copy).then_inc(x2hi_done, 1)

            squares(0)
            expert_high(0, range(KC))
            act.wait_ge(ln_done, 1)
            act.wait_ge(walk_done, 2)
            normalise(0)
            x_high(0)

            def step(s, lo):
                prev, nxt, ln2 = lo >= 1, lo < STEPS - 1, lo >= LN2_LAG
                if lo + 1 < E:
                    squares(lo + 1)
                e = a.value_load(walk[0:1, 0, ds(s, 1)], min_val=0, max_val=E - 1)
                if nxt:
                    t = a.value_load(walk[0:1, 1, ds(s + 1, 1)], min_val=0, max_val=TILES - 1)
                if prev:
                    act.wait_ge(hT_done, s)
                    if lo >= 2:
                        act.wait_ge(y_done, s - 1)
                    a.activation(hTh[:], HT[:], ACT.Copy).then_inc(hhi_done, 1)
                if lo < PAIRS:
                    act.wait_ge(w_in[lo % 2], 8 * (s - lo % 2) + 16)
                    if lo >= 2:
                        act.wait_ge(q_done, s - 1)
                    a.activation(w_big[:, lo % 2], ws[:, lo % 2], ACT.Abs, scale=FP8_STEP).then_inc(abs_done, 1)
                if nxt:
                    act.wait_ge(ln_done, s + 2)
                    act.wait_ge(xT_done, s + 1)
                    normalise(t)
                if ln2:
                    normalise2(s - LN2_LAG, s + 2)
                if lo + 1 < E:
                    expert_high(lo + 1, (0, 1))
                act.wait_ge(z_done, s + 1)
                if prev:
                    act.wait_ge(h_done, s)
                a.activation(silu_z[:], Z[:], ACT.Silu, scale=z_scale[:, ds(e, 1)]).then_inc(silu_done, 1)
                if lo + 1 < E:
                    expert_high(lo + 1, (2, 3))
                if nxt:
                    x_high(s + 1)
                if ln2:
                    x2_high(s - LN2_LAG, X2T)
                if lo < GU_PAIRS:
                    act.wait_ge(q_done, s + 1)
                    if prev:
                        act.wait_ge(norm_done, s)
                    a.activation(sq[:], W8[:, ds(2 * s, 2), :], ACT.Square).then_inc(q_used, 1)
                elif lo < PAIRS:
                    if lo == GU_PAIRS:
                        act.wait_ge(fscale_done, 1)
                    act.wait_ge(q_done, s + 1)
                    for i in range(2):
                        ins = a.activation(W8[:, ds(2 * s + i, 1), :].rearrange("p a n -> p (a n)"), qd[:, i, :],
                                           ACT.Copy, scale=f_inv[:, ds(2 * (s - GU_PAIRS) + i, 1)])
                    ins.then_inc(q_used, 1)

            for s in range(6):
                step(s, s)
            with act.Fori(3, 6) as half:
                step(2 * half, 6)
                step(2 * half + 1, 7)
            with act.Fori(6, 9) as half:
                step(2 * half, 12)
                step(2 * half + 1, 13)
            step(STEPS - 1, STEPS - 1)

            def last_h_high():
                act.wait_ge(hT_done, STEPS)
                act.wait_ge(y_done, STEPS - 1)
                a.activation(hTh[:], HT[:], ACT.Copy).then_inc(hhi_done, 1)

            def gate_silu(g, c):
                act.wait_ge(gate_done, g * IC + c + 1)
                if not (isinstance(g, int) and g * IC + c < 2):
                    act.wait_ge(fuse_done, g * IC + c - 1)
                a.activation(sg[:, c % 2, :], GATE[c % 2][:], ACT.Silu,
                             scale=gate_mul[:, c:c + 1]).then_inc(sg_done, 1)

            def fuse_high(g, c):
                act.wait_ge(fuse_done, g * IC + c + 1)
                if not (isinstance(g, int) and g * IC + c < 2):
                    act.wait_ge(down_done, g * IC + c - 1)
                a.activation(fh[:, c % 2, :], fuse[:, c % 2, :], ACT.Copy).then_inc(fh_done, 1)

            last_h_high()
            normalise2(TILES - 2, STEPS + 2)
            x2_high(TILES - 2, XT)
            gate_silu(0, 0)
            normalise2(TILES - 1, STEPS + 3)
            fuse_high(0, 0)
            x2_high(TILES - 1, XT)

            gate_silu(0, 1)
            fuse_high(0, 1)

            def group(g, last):
                for c in range(2, IC):
                    gate_silu(g, c)
                    fuse_high(g, c)
                if not last:
                    for c in range(2):
                        gate_silu(g + 1, c)
                        fuse_high(g + 1, c)

            with act.Fori(0, GROUPS - 1) as gi:
                group(gi, False)
            group(GROUPS - 1, True)

        @block.vector
        def _(dve):
            v = nc.vector
            chained = [0]

            def link(ins, s_, count):
                count[0] += 1
                ins.then_inc(s_, 1)
                dve.wait_ge(s_, count[0])

            dve.wait_ge(ids_in, 16)
            dve.wait_ge(consts, N_CONSTS)
            link(v.tensor_copy(idf[:], ids[:]), sort_v, chained)
            for j in range(1, E):
                ins = v.tensor_scalar(cge[:, j], idf[:], float((E - j) * PER_EXPERT), None, ALU.is_ge)
            link(ins, sort_v, chained)
            v.tensor_tensor(onehot[:], cge[:, 1:E + 1, :].rearrange("p e c -> p (e c)"),
                            cge[:, 0:E, :].rearrange("p e c -> p (e c)"), ALU.subtract).then_inc(onehot_done, 1)
            dve.wait_ge(counts_done, 1)
            link(v.tensor_copy(total[:], SMALL[:, 64:128]), sort_v, chained)
            link(v.tensor_tensor_scan(incl[:], ones64[:], total[:], 0.0, ALU.mult, ALU.add), sort_v, chained)
            link(v.tensor_tensor(base[:], incl[:], total[:], ALU.subtract), sort_v, chained)
            link(v.tensor_tensor(rank_e[:], SMALL[:, 0:64], base[:], ALU.add), sort_v, chained)
            link(v.tensor_tensor(rank_m[:], rank_e[:], onehot[:], ALU.mult), sort_v, chained)
            link(v.tensor_reduce(rank[:], rank_m[:].rearrange("p (e c) -> p c e", e=E), AX.X, ALU.add),
                 sort_v, chained)
            link(v.tensor_copy(rank_i[:], rank[:]), sort_v, chained)
            v.tensor_scalar(tile_i[:], rank_i[:], 7, None, ALU.arith_shift_right)
            link(v.tensor_scalar(row_i[:], rank_i[:], P - 1, None, ALU.bitwise_and), sort_v, chained)
            v.tensor_copy(row_f[:], row_i[:])
            v.tensor_copy(tile_f[:], tile_i[:]).then_inc(place_done, 1)
            dve.wait_ge(place_done, 1)
            v.tensor_tensor(tile_eq[:], iota_q[:, 0:TILES].unsqueeze(1).to_broadcast([P, TILES, TILES]),
                            tile_f[:].unsqueeze(2).to_broadcast([P, TILES, TILES]),
                            ALU.is_equal).then_inc(tile_eq_done, 1)
            v.tensor_tensor(row_hot[:], iota_q[:].unsqueeze(1).to_broadcast([P, TILES, P]),
                            row_f[:].unsqueeze(2).to_broadcast([P, TILES, P]), ALU.is_equal).then_inc(row_hot_done, 1)
            dve.wait_ge(order_mm, 1)
            v.tensor_copy(order[:], SMALL[:, 128:128 + TILES]).then_inc(order_done, 1)

            def expert_rows(e):
                dve.wait_ge(ssq_done, KC * (e + 1))
                v.tensor_reduce(row_max[:, e:e + 1], row_ssq[:, e, :], AX.X, ALU.max).then_inc(rmax_done, 1)

            expert_rows(0)

            starts = [base[:, e * TILES:e * TILES + 1] for e in range(1, E)]
            for e in range(1, E):
                ins = v.tensor_scalar(bound[:, e - 1:e], starts[e - 1], float(TOK - 1), None, ALU.min)
            link(ins, sort_v, chained)
            for e in range(1, E):
                ins = v.tensor_scalar(past[:, e - 1], step128[:], float(P - P * e), bound[:, e - 1:e],
                                      ALU.add, ALU.is_gt)
            link(ins, sort_v, chained)
            link(v.tensor_tensor(past2[:], past[:, 0], past[:, 1], ALU.add), sort_v, chained)
            link(v.tensor_tensor(e_of[:], past2[:], past[:, 2], ALU.add), sort_v, chained)
            v.scalar_tensor_tensor(out=walk_f[:], in0=e_of[:], scalar=-float(P), in1=step128[:],
                                   op0=ALU.mult, op1=ALU.add)
            link(v.scalar_tensor_tensor(out=pos[:], in0=e_of[:], scalar=-float(P), in1=step_pos[:],
                                        op0=ALU.mult, op1=ALU.add), sort_v, chained)
            v.tensor_copy(walk[:, 0], e_of[:])
            v.tensor_scalar(walk[:, 1], walk_f[:], 1.0 / P, None, ALU.mult).then_inc(walk_done, 1)
            for e in range(1, E):
                ins = v.tensor_scalar(cnt[:, e - 1], pos[:], starts[e - 1], None, ALU.is_ge)
            link(ins, sort_v, chained)
            link(v.tensor_tensor(cnt2[:], cnt[:, 0], cnt[:, 1], ALU.add), sort_v, chained)
            link(v.tensor_tensor(cnt3[:], cnt2[:], cnt[:, 2], ALU.add), sort_v, chained)
            v.tensor_tensor(mask[:], cnt3[:], e_of[:], ALU.is_equal).then_inc(walk_done, 1)

            dve.wait_ge(tanh_done, 2)
            v.tensor_scalar(tgx24[:], tgx[:], 2.0 ** 24, None, ALU.mult).then_inc(gates_done, 1)
            v.tensor_scalar(dsb[:], dsc[:], tgf[:, 0:1], None, ALU.mult).then_inc(gates_done, 1)
            dve.wait_ge(gates_done, 2)

            dve.wait_ge(scales_T, 1)
            v.tensor_copy(gs[:], SMALL[:, 160:160 + IC])
            v.tensor_copy(us[:], SMALL[:, 176:176 + IC]).then_inc(scales_done, 1)

            mcount = [0]

            def expert_scale(e):
                c = slice(e, e + 1)
                dve.wait_ge(ninv_done, e + 1)
                link(v.tensor_scalar(m_scale[:, c].bitcast(I32), n_top[:, c].bitcast(I32), POW2_MASK, None,
                                     ALU.bitwise_and), mchain, mcount)
                link(v.reciprocal(m_inv[:, c], m_scale[:, c]), mchain, mcount)
                v.tensor_scalar(z_scale[:, c], m_inv[:, c], 1.0 / X_SCALE, None, ALU.mult)
                v.tensor_scalar(h_scale[:, c], m_scale[:, c], 2.0 ** -24 / X_SCALE, None, ALU.mult)
                link(v.tensor_tensor(m_inv2[:, c], m_inv[:, c], m_inv[:, c], ALU.mult), mchain, mcount)
                v.scalar_tensor_tensor(out=y_scale[:, c], in0=m_inv2[:, c], scalar=tgx24[:, 0:1], in1=m_inv[:, c],
                                       op0=ALU.mult, op1=ALU.mult).then_inc(mscale_done, 1)

            def expert_low(e, chunks):
                dve.wait_ge(mscale_done, e + 1)
                for k in chunks:
                    w = slice((e * KC + k) * 512, (e * KC + k + 1) * 512)
                    dve.wait_ge(mhi_done, KC * e + k + 1)
                    v.scalar_tensor_tensor(out=Ml[:, w], in0=MT[k % 2][:], scalar=m_scale[:, e:e + 1],
                                           in1=Mh[:, w], op0=ALU.mult, op1=ALU.subtract).then_inc(mlo_done, 1)

            def tile_stats(which, tile):
                src = xs[:, tile, :] if isinstance(tile, int) else xs[:, ds(tile, 1), :].rearrange("p a d -> p (a d)")
                return v.bn_stats(stats[:, which, :], src)

            def aggregate(n, lo, hi):
                dve.wait_ge(stats_done, n + 1)
                dve.nop(nofuse=True)
                for i in range(lo, hi):
                    ins = v.bn_aggr(mv[:, i, :], stats[:, i, :])
                ins.then_inc(mv_done, 1)

            def low_part(dst, src, high, ready, n, done):
                dve.wait_ge(ready, n)
                v.tensor_tensor(dst, src, high, ALU.subtract).then_inc(done, 1)

            dve.wait_ge(gathered[0], 16)
            tile_stats(0, 0).then_inc(stats_done, 1)
            aggregate(0, 0, 1)
            expert_scale(0)
            expert_low(0, range(KC))
            low_part(xTl[:], XT[:], xTh[:], xhi_done, 1, xlo_done)

            def step(s, lo):
                prev, nxt, ln2 = lo >= 1, lo < STEPS - 1, lo >= LN2_LAG
                e = v.value_load(walk[0:1, 0, ds(s, 1)], min_val=0, max_val=E - 1)
                if nxt:
                    t = v.value_load(walk[0:1, 1, ds(s + 1, 1)], min_val=0, max_val=TILES - 1)
                if prev:
                    tp = v.value_load(walk[0:1, 1, ds(s - 1, 1)], min_val=0, max_val=TILES - 1)
                if lo == 0:
                    dve.wait_ge(gathered[1], 48)
                if lo == 3:
                    dve.wait_ge(gathered[2], 16 * (TILES - 4))
                if lo >= 2:
                    dve.wait_ge(x1_done, s - 1)
                dve.wait_ge(ln_done, s + 1)
                if nxt:
                    ins = tile_stats(0, t)
                if ln2:
                    ins = tile_stats(1, s - LN2_LAG)
                ins.then_inc(stats_done, 1)
                aggregate(s + 1, 0 if nxt else 1, 2 if ln2 else 1)
                if lo + 1 < E:
                    expert_rows(lo + 1)
                if prev:
                    if lo >= 2:
                        dve.wait_ge(y_done, s - 1)
                    low_part(hTl[:], HT[:], hTh[:], hhi_done, s, hlo_done)
                if lo < PAIRS:
                    dve.wait_ge(abs_done, s + 1)
                    v.tensor_scalar(w_big[:, lo % 2], w_big[:, lo % 2], FP8_FLOOR, None,
                                    ALU.max).then_inc(big_done, 1)
                if lo + 1 < E:
                    expert_scale(lo + 1)
                    expert_low(lo + 1, (0, 1))
                dve.wait_ge(silu_done, s + 1)
                if prev:
                    dve.wait_ge(hT_done, s)
                v.scalar_tensor_tensor(out=h[:], in0=Z[:], scalar=h_scale[:, ds(e, 1)], in1=silu_z[:],
                                       op0=ALU.mult, op1=ALU.mult).then_inc(h_done, 1)
                if lo + 1 < E:
                    expert_low(lo + 1, (2, 3))
                if nxt:
                    low_part(xTl[:], XT[:], xTh[:], xhi_done, s + 2, xlo_done)
                if ln2:
                    low_part(x2_part(s - LN2_LAG, 1), X2T[:].rearrange("p (k i) -> p k i", k=KC),
                             x2_part(s - LN2_LAG, 0), x2hi_done, s - LN2_LAG + 1, x2lo_done)
                if prev:
                    add_expert(s - 1, tp, s + 2 if nxt else None)

            def add_expert(s, tile, xn_reads):
                dve.wait_ge(y_done, s + 1)
                dve.wait_ge(rows_done, s + 1)
                if xn_reads is not None:
                    dve.wait_ge(xn_done, xn_reads)
                row = xs[:, ds(tile, 1), :].rearrange("p a d -> p (a d)")
                v.scalar_tensor_tensor(out=row, in0=Y[:], scalar=row_scale[:, ds(s, 1)], in1=row,
                                       op0=ALU.mult, op1=ALU.add).then_inc(x1_done, 1)

            for s in range(6):
                step(s, s)
            with dve.Fori(3, 6) as half:
                step(2 * half, 6)
                step(2 * half + 1, 7)

            fcount = [0]
            dve.wait_ge(scales_done, 1)
            dve.wait_ge(norm_done, GU_PAIRS)
            norms = SMALL[:, 0:2 * THIRDS * KC * KC].rearrange("p (m k j) -> p m j k", k=KC, j=KC)
            link(v.tensor_reduce(col_ssq[:].rearrange("p w (a j) -> p (w a) j", j=KC), norms, AX.X, ALU.add),
                 fchain, fcount)
            v.tensor_tensor(nn[:], col_ssq[:, 0, :], col_ssq[:, 1, :], ALU.mult)
            link(v.tensor_tensor(gu[:], gs[:], us[:], ALU.mult), fchain, fcount)
            link(v.tensor_tensor(gu2[:], gu[:], gu[:], ALU.mult), fchain, fcount)
            link(v.tensor_tensor(b2[:], nn[:], gu2[:], ALU.mult), fchain, fcount)
            v.tensor_scalar(b2c[:], b2[:], 1e-30, 1e38, ALU.max, ALU.min).then_inc(b2_done, 1)
            dve.wait_ge(binv_done, 1)
            link(v.tensor_scalar(f_scale[:].bitcast(I32), f_top[:].bitcast(I32), POW2_MASK, None,
                                 ALU.bitwise_and), fchain, fcount)
            v.tensor_scalar(gate_mul[:], gs[:], 1.0 / X_SCALE, None, ALU.mult)
            link(v.tensor_scalar(up_mul0[:], us[:], 1.0 / X_SCALE, None, ALU.mult), fchain, fcount)
            v.tensor_tensor(up_mul[:], up_mul0[:], f_scale[:], ALU.mult)
            v.reciprocal(f_inv[:], f_scale[:]).then_inc(fscale_done, 1)

            with dve.Fori(6, 9) as half:
                step(2 * half, 12)
                step(2 * half + 1, 13)
            step(STEPS - 1, STEPS - 1)

            low_part(hTl[:], HT[:], hTh[:], hhi_done, STEPS, hlo_done)
            dve.wait_ge(ln_done, STEPS + 1)
            dve.wait_ge(x1_done, STEPS - 1)
            tile_stats(1, TILES - 2).then_inc(stats_done, 1)
            aggregate(STEPS + 1, 1, 2)
            low_part(x2_part(TILES - 2, 1), XT[:].rearrange("p (k i) -> p k i", k=KC),
                     x2_part(TILES - 2, 0), x2hi_done, TILES - 1, x2lo_done)
            tl = v.value_load(walk[0:1, 1, STEPS - 1:STEPS], min_val=0, max_val=TILES - 1)
            add_expert(STEPS - 1, tl, None)
            dve.wait_ge(ln_done, STEPS + 2)
            dve.wait_ge(x1_done, STEPS)
            tile_stats(1, TILES - 1).then_inc(stats_done, 1)
            aggregate(STEPS + 2, 1, 2)

            def ffn_unit(g, c):
                u = g * IC + c
                dve.wait_ge(up_done, u + 1)
                dve.wait_ge(sg_done, u + 1)
                if not (isinstance(g, int) and g * IC + c < 2):
                    dve.wait_ge(fl_done, u - 1)
                v.scalar_tensor_tensor(out=fuse[:, c % 2, :], in0=UP[c % 2][:], scalar=up_mul[:, c:c + 1],
                                       in1=sg[:, c % 2, :], op0=ALU.mult, op1=ALU.mult).then_inc(fuse_done, 1)
                if not (isinstance(g, int) and g * IC + c < 2):
                    dve.wait_ge(down_done, u - 1)
                dve.wait_ge(fh_done, u + 1)
                v.tensor_tensor(fl[:, c % 2, :], fuse[:, c % 2, :], fh[:, c % 2, :],
                                ALU.subtract).then_inc(fl_done, 1)

            ffn_unit(0, 0)
            dve.wait_ge(x2hi_done, TILES)
            v.tensor_tensor(x2_part(TILES - 1, 1), XT[:].rearrange("p (k i) -> p k i", k=KC),
                            x2_part(TILES - 1, 0), ALU.subtract).then_inc(acc_free, TPG)

            ffn_unit(0, 1)

            def group(g, last):
                for c in range(2, IC):
                    ffn_unit(g, c)
                if not last:
                    ffn_unit(g + 1, 0)
                for t in range(TPG):
                    if t < TPG - 1:
                        dve.wait_ge(acc_done, g * (TPG - 1) + t + 1)
                    else:
                        dve.wait_ge(down_done, g * IC + IC)
                    v.tensor_tensor(slab_tile(g, t), ACC[t][:], dsb[:], ALU.mult).then_inc(acc_free, 1)
                if not last:
                    ffn_unit(g + 1, 1)

            with dve.Fori(0, GROUPS - 1) as gi:
                group(gi, False)
            group(GROUPS - 1, True)

        @block.tensor
        def _(pe):
            t_ = nc.tensor

            def transpose4(dst, src, done):
                for k in range(KC):
                    ins = t_.matmul(dst[:, k * P:(k + 1) * P], src[:, k * P:(k + 1) * P], ident[:],
                                    is_transpose=True, start=(k == 0), stop=(k == KC - 1))
                ins.then_inc(done, 1)

            pe.wait_ge(consts, N_CONSTS)
            pe.wait_ge(onehot_done, 1)
            t_.matmul(SMALL[:, 0:64], below[:], onehot[:], start=True, stop=True)
            t_.matmul(SMALL[:, 64:128], ones[:], onehot[:], start=True, stop=True).then_inc(counts_done, 1)

            def expert_turn(e, chunks):
                pe.wait_ge(ctx_in[e % 2], 16 * (e // 2 + 1))
                for k in chunks:
                    if KC * e + k >= 2:
                        pe.wait_ge(mlo_done, KC * e + k - 1)
                    for r in range(KC):
                        ins = t_.matmul(MT[k % 2][:, r * P:(r + 1) * P], cs[:, e % 2, r, k * P:(k + 1) * P],
                                        ident[:], is_transpose=True, start=(r == 0), stop=(r == KC - 1))
                    ins.then_inc(mT_done, 1)

            pe.wait_ge(row_hot_done, 1)
            pe.wait_ge(tile_tok_done, 1)
            for c in range(TILES):
                ins = t_.matmul(SMALL[:, 128:128 + TILES], row_hot[:, c, :], tile_tok[:, c, :],
                                start=(c == 0), stop=(c == TILES - 1))
            ins.then_inc(order_mm, 1)
            pe.wait_ge(params_in, 80)
            pe.wait_ge(order_done, 1)
            t_.matmul(SMALL[:, 160:160 + IC], gs_rows[:], ident[0:IC, 0:IC], is_transpose=True, start=True, stop=True)
            t_.matmul(SMALL[:, 176:176 + IC], us_rows[:], ident[0:IC, 0:IC], is_transpose=True, start=True,
                      stop=True).then_inc(scales_T, 1)
            expert_turn(0, range(KC))
            pe.wait_ge(xn_done, 1)
            transpose4(XT, xn, xT_done)
            pe.wait_ge(walk_done, 2)

            def product(dst, e, high, low, done):
                n = 0
                for k in range(KC):
                    mh = Mh[:, ds(e * (KC * 512) + k * 512, 512)]
                    ml = Ml[:, ds(e * (KC * 512) + k * 512, 512)]
                    for lhs, rhs in ((high, mh), (high, ml), (low, mh)):
                        ins = t_.matmul(dst[:], lhs[:, k * P:(k + 1) * P], rhs, start=(n == 0), stop=(n == 3 * KC - 1))
                        n += 1
                ins.then_inc(done, 1)

            def turn_h(s):
                pe.wait_ge(h_done, s + 1)
                transpose4(HT, h, hT_done)

            def turn_x2(tile, dst):
                pe.wait_ge(x2n_done, tile + 1)
                if not (isinstance(tile, int) and tile == 0):
                    pe.wait_ge(x2lo_done, tile)
                transpose4(dst, x2n, x2T_done)

            def product_y(s):
                e = t_.value_load(walk[0:1, 0, ds(s, 1)], min_val=0, max_val=E - 1)
                pe.wait_ge(hlo_done, s + 1)
                if not (isinstance(s, int) and s == 0):
                    pe.wait_ge(x1_done, s)
                product(Y, e, hTh, hTl, y_done)

            def step(s, lo):
                if lo >= 1:
                    if lo >= 2:
                        pe.wait_ge(hlo_done, s - 1)
                    turn_h(s - 1)
                if lo + 1 < E:
                    expert_turn(lo + 1, (0, 1))
                e = t_.value_load(walk[0:1, 0, ds(s, 1)], min_val=0, max_val=E - 1)
                pe.wait_ge(xlo_done, s + 1)
                pe.wait_ge(mlo_done, KC * (min(lo, E - 1) + 1))
                product(Z, e, xTh, xTl, z_done)
                if lo + 1 < E:
                    expert_turn(lo + 1, (2, 3))
                if lo < STEPS - 1:
                    pe.wait_ge(xn_done, s + 2)
                    transpose4(XT, xn, xT_done)
                if lo >= LN2_LAG:
                    turn_x2(s - LN2_LAG, X2T)
                if 1 <= lo <= GU_PAIRS:
                    norms(s - 1)
                if lo >= 1:
                    product_y(s - 1)

            def norms(n):
                pe.wait_ge(q_used, n + 1)
                if isinstance(n, int) and n == 0:
                    pe.wait_ge(scales_done, 1)
                for i in range(2):
                    for j in range(KC):
                        ins = t_.matmul(SMALL[:, ds(2 * KC * n + i * KC + j, 1)], sq[:, i, j * P:(j + 1) * P],
                                        ones[:, 0:1], start=True, stop=True)
                ins.then_inc(norm_done, 1)

            for s in range(6):
                step(s, s)
            with pe.Fori(3, 6) as half:
                step(2 * half, 6)
                step(2 * half + 1, 7)
            norms(GU_PAIRS - 1)
            with pe.Fori(6, 9) as half:
                step(2 * half, 13)
                step(2 * half + 1, 14)
            step(STEPS - 1, STEPS - 1)

            def gate_up(g, c):
                a, j = c // KC, c % KC
                for dst, first, free, done in ((GATE, 0, sg_done, gate_done), (UP, IC, fuse_done, up_done)):
                    if not (isinstance(g, int) and g * IC + c < 2):
                        pe.wait_ge(free, g * IC + c - 1)
                    for k in range(KC):
                        w = W8[:, first + a * KC + k, j * P:(j + 1) * P]
                        for part in range(2):
                            ins = t_.matmul(dst[c % 2][:], w, x2_group(g, part, k), start=(k == 0 and part == 0),
                                            stop=(k == KC - 1 and part == 1))
                    ins.then_inc(done, 1)

            def down(g, c):
                pe.wait_ge(fl_done, g * IC + c + 1)
                for t in range(TPG):
                    if c == 0:
                        pe.wait_ge(acc_free, g * TPG + t + 1)
                    for part in (fh, fl):
                        ins = t_.matmul(ACC[t][:], part[:, c % 2, t * P:(t + 1) * P], W8[:, 2 * IC + c, :],
                                        start=(c == 0 and part is fh), stop=(c == IC - 1 and part is fl))
                    if c == IC - 1 and t < TPG - 1:
                        ins.then_inc(acc_done, 1)
                ins.then_inc(down_done, 1)

            pe.wait_ge(hlo_done, STEPS - 1)
            turn_h(STEPS - 1)
            pe.wait_ge(fscale_done, 1)
            pe.wait_ge(xlo_done, STEPS)
            turn_x2(TILES - 2, XT)
            product_y(STEPS - 1)
            pe.wait_ge(q_used, PAIRS)
            gate_up(0, 0)
            turn_x2(TILES - 1, XT)
            gate_up(0, 1)
            down(0, 0)

            def group(g, last):
                for c in range(2, IC):
                    gate_up(g, c)
                    down(g, c - 1)
                if not last:
                    gate_up(g + 1, 0)
                down(g, IC - 1)
                if not last:
                    gate_up(g + 1, 1)
                    down(g + 1, 0)

            with pe.Fori(0, GROUPS - 1) as gi:
                group(gi, False)
            group(GROUPS - 1, True)


_INS = ["x", "itok_BxS_13_99985", "ctx_2048", "g_xattn", "g_ffn", "L0_ffn_gate_w", "L0_ffn_up_w", "L0_ffn_down_w",
        "L0_ffn_gate_scale", "L0_ffn_up_scale", "L0_ffn_down_scale"]


def kernel(**inputs):
    import numpy as np
    import concourse.bacc as bacc
    from concourse.bass_utils import run_bass_kernel_spmd as run

    nc = bacc.Bacc("TRN2", target_bir_lowering=False, num_devices=1)
    arrays, args = {}, []
    for name in _INS:
        a = np.ascontiguousarray(inputs[name])
        arrays["in_" + name] = a
        args.append(nc.dram_tensor("in_" + name, a.shape, mybir.dt.from_np(a.dtype), kind="ExternalInput").ap())
    args.append(nc.dram_tensor("out_0", inputs["x"].shape, mybir.dt.float32, kind="ExternalOutput").ap())
    build(nc, *args)
    r = run(nc, [arrays], core_ids=[0])
    return r.results[0]["out_0"]
```

```python
from contextlib import ExitStack

import concourse.bass as bass
from concourse import mybir

F32, F16, BF16, I32 = mybir.dt.float32, mybir.dt.float16, mybir.dt.bfloat16, mybir.dt.int32
ALU = mybir.AluOpType
ACT = mybir.ActivationFunctionType
AX = mybir.AxisListType
RMAX = bass.bass_isa.ReduceOp.max
ds = bass.ds

P = 128
LN_EPS = 1e-5
VOCAB, EXPERTS = 25000, 4
PER_EXPERT = VOCAB // EXPERTS
X_SCALE = 2.0 ** 11
POW2_MASK = 0x7F800000
FP8_STEP = 2.0 ** 20
FP8_FLOOR = FP8_STEP * 2.0 ** -6 * (1 + 2.0 ** -19)


def build(nc, x, token_ids, ctx, g_xattn, g_ffn, gate_w, up_w, down_w, gate_scale, up_scale, down_scale, out):
    B, S, D = x.shape
    TOK = B * S
    TILES = TOK // P
    E = ctx.shape[0]
    KC = D // P
    INNER = gate_w.shape[1]
    IC = INNER // P
    STEPS = TILES + E - 1
    GROUPS = TOK // 512
    TPG = TILES // GROUPS
    THIRDS = INNER // 512
    PAIRS = 3 * IC // 2
    GU_PAIRS = 2 * IC // 2
    STATS1_LEAD = 4
    STATS2_LAG = 5
    X2_LAG = 6
    NORM_LAG = 2
    ROUNDS = TILES + STATS1_LEAD + STATS2_LAG
    assert E == EXPERTS and KC == 4 and D == 512 and PAIRS == STEPS - 1

    x_rows = x.rearrange("b s d -> (b s) d")
    out_rows = out.rearrange("b s d -> (b s) d")
    ids_v = token_ids.rearrange("b s -> (b s)").rearrange("(p c) -> p c", c=TILES)
    ctx_v = ctx.rearrange("e (r p) d -> e p r d", p=P)
    gate_v = gate_w.rearrange("(k p) n -> p k n", p=P)
    up_v = up_w.rearrange("(k p) n -> p k n", p=P)
    down_v = down_w.rearrange("(k p) n -> p k n", p=P)

    with ExitStack() as stack:
        def sb(name, shape, dt):
            return stack.enter_context(nc.sbuf_tensor(name, shape, dt))

        def sem(name):
            return stack.enter_context(nc.semaphore(name))

        xs = sb("xs", [P, TILES, D], F32)
        Mh = sb("Mh", [P, E * KC * 512], F16)
        Ml = sb("Ml", [P, E * KC * 512], F16)
        X2 = sb("X2", [P, GROUPS, 2, KC, TPG, P], F16)
        W8 = sb("W8", [P, 3 * IC, 512], BF16)
        cs = sb("cs", [P, 2, KC, D], F32)
        ws = sb("ws", [P, 2, 2, 512], F32)
        w_big = sb("w_big", [P, 2, 2, 512], F32)
        w_sum = sb("w_sum", [P, 2, 512], F32)
        sq = sb("sq", [P, 2, 512], BF16)
        junk = sb("junk", [P, KC * D], BF16)
        warm = sb("warm", [P, 1], F32)
        xn = sb("xn", [P, D], F32)
        x2n = sb("x2n", [P, D], F32)
        xTh = sb("xTh", [P, KC * P], F16)
        xTl = sb("xTl", [P, KC * P], F16)
        hTh = sb("hTh", [P, KC * P], F16)
        hTl = sb("hTl", [P, KC * P], F16)
        silu_z = sb("silu_z", [P, 512], F32)
        h = sb("h", [P, 512], F32)
        sg = cs[:, 0, 0:2, :]
        fuse = cs[:, 0, 2:4, :]
        fh = cs[:, 1, 0:1, :].rearrange("p a n -> p (a n)").bitcast(F16).rearrange("p (b n) -> p b n", b=2)
        fl = cs[:, 1, 1:2, :].rearrange("p a n -> p (a n)").bitcast(F16).rearrange("p (b n) -> p b n", b=2)
        ident = sb("ident", [P, P], F32)
        zero = sb("zero", [P, P], F32)
        below = sb("below", [P, P], BF16)
        ones = sb("ones", [P, P], BF16)
        iota_q = sb("iota_q", [P, P], F32)
        tok_no = sb("tok_no", [P, TILES], F32)
        step128 = sb("step128", [P, STEPS], F32)
        step_pos = sb("step_pos", [P, STEPS], F32)
        ones64 = sb("ones64", [P, E * TILES], F32)
        ln_eps = sb("ln_eps", [P, 3, 2], F32)
        ln_half = sb("ln_half", [P, 3, 2], F32)
        ln_zero = sb("ln_zero", [P, 3, 2], F32)
        mhalf = sb("mhalf", [P, IC], F32)
        ids = sb("ids", [P, TILES], I32)
        idf = sb("idf", [P, TILES], F32)
        cge = sb("cge", [P, E + 1, TILES], F32)
        onehot = sb("onehot", [P, E * TILES], BF16)
        total = sb("total", [P, E * TILES], F32)
        incl = sb("incl", [P, E * TILES], F32)
        base = sb("base", [P, E * TILES], F32)
        rank_e = sb("rank_e", [P, E * TILES], F32)
        rank_m = sb("rank_m", [P, E * TILES], F32)
        rank = sb("rank", [P, TILES], F32)
        rank_i = sb("rank_i", [P, TILES], I32)
        row_i = sb("row_i", [P, TILES], I32)
        tile_i = sb("tile_i", [P, TILES], I32)
        row_f = sb("row_f", [P, TILES], F32)
        tile_f = sb("tile_f", [P, TILES], F32)
        row_hot = sb("row_hot", [P, TILES, P], F16)
        tile_eq = sb("tile_eq", [P, TILES, TILES], F32)
        tile_tok = sb("tile_tok", [P, TILES, TILES], F16)
        order = sb("order", [P, TILES], I32)
        bound = sb("bound", [P, E - 1], F32)
        past = sb("past", [P, E - 1, STEPS], F32)
        past2 = sb("past2", [P, STEPS], F32)
        e_of = sb("e_of", [P, STEPS], F32)
        pos = sb("pos", [P, STEPS], F32)
        cnt = sb("cnt", [P, E - 1, STEPS], F32)
        cnt2 = sb("cnt2", [P, STEPS], F32)
        cnt3 = sb("cnt3", [P, STEPS], F32)
        mask = sb("mask", [P, STEPS], F32)
        last_f = sb("last_f", [P, 1], F32)
        walk_last = sb("walk_last", [P, 1], I32)
        tile_of = sb("tile_of", [P, STEPS], F32)
        walk_f = sb("walk_f", [P, STEPS], F32)
        walk = sb("walk", [P, STEPS], I32)
        gx = sb("gx", [P, 1], F32)
        gf = sb("gf", [P, 1], F32)
        tgx = sb("tgx", [P, 1], F32)
        tgf = sb("tgf", [P, 1], F32)
        tgx24 = sb("tgx24", [P, 1], F32)
        gs_rows = sb("gs_rows", [IC, P], F32)
        us_rows = sb("us_rows", [IC, P], F32)
        gs = sb("gs", [P, IC], F32)
        us = sb("us", [P, IC], F32)
        dsc = sb("dsc", [P, D], F32)
        dsb = sb("dsb", [P, D], F32)
        part_ssq = sb("part_ssq", [P, E], F32)
        all_max = sb("all_max", [P, E], F32)
        n2 = sb("n2", [P, E], F32)
        n_inv = sb("n_inv", [P, E], F32)
        n_top = sb("n_top", [P, E], F32)
        m_scale = sb("m_scale", [P, E], F32)
        m_inv = sb("m_inv", [P, E], F32)
        m_inv2 = sb("m_inv2", [P, E], F32)
        z_scale = sb("z_scale", [P, E], F32)
        h_scale = sb("h_scale", [P, E], F32)
        y_scale = sb("y_scale", [P, E], F32)
        stats = sb("stats", [P, 4, 2, 6], F32)
        mv = sb("mv", [P, 4, 2, 2], F32)
        var_eps = sb("var_eps", [P, ROUNDS, 2], F32)
        mean_r = sb("mean_r", [P, ROUNDS, 2], F32)
        ln_tab = sb("ln_tab", [P, ROUNDS, 2, 2], F32)
        step_ln = sb("step_ln", [P, STEPS, 2], F32)
        col_ssq = sb("col_ssq", [P, 2, IC], F32)
        gu = sb("gu", [P, IC], F32)
        gu2 = sb("gu2", [P, IC], F32)
        nn = sb("nn", [P, IC], F32)
        b2 = sb("b2", [P, IC], F32)
        b2c = sb("b2c", [P, IC], F32)
        b_inv = sb("b_inv", [P, IC], F32)
        f_top = sb("f_top", [P, IC], F32)
        f_scale = sb("f_scale", [P, IC], F32)
        f_inv = sb("f_inv", [P, IC], F32)
        gate_mul = sb("gate_mul", [P, IC], F32)
        up_mul0 = sb("up_mul0", [P, IC], F32)
        up_mul = sb("up_mul", [P, IC], F32)

        bank = [stack.enter_context(nc.psum_tensor(f"bank{i}", [P, 512], F32)) for i in range(8)]
        Z, HT, XT, Y, X2T, SMALL = bank[0], bank[1], bank[2], bank[3], bank[4], bank[6]
        MT = [bank[5], bank[7]]
        MT_FIRST = [bank[5], bank[7], bank[0], bank[1]]
        ACC = [bank[0], bank[1], bank[2], bank[3]]
        GATE = [bank[5], bank[7]]
        UP = [bank[6], bank[4]]

        consts = sem("consts")
        ids_in = sem("ids_in")
        params_in = sem("params_in")
        ctx_in = [sem("ctx_in0"), sem("ctx_in1")]
        w_in = [sem("w_in0"), sem("w_in1")]
        sort_v = sem("sort_v")
        onehot_done = sem("onehot_done")
        counts_done = sem("counts_done")
        place_done = sem("place_done")
        row_hot_done = sem("row_hot_done")
        tile_eq_done = sem("tile_eq_done")
        tile_tok_done = sem("tile_tok_done")
        order_mm = sem("order_mm")
        order_done = sem("order_done")
        gathered = [sem(f"gathered{i}") for i in range(5)]
        walk_done = sem("walk_done")
        scales_T = sem("scales_T")
        scales_done = sem("scales_done")
        tanh_done = sem("tanh_done")
        gates_done = sem("gates_done")
        ssq_done = sem("ssq_done")
        pool_m = sem("pool_m")
        ninv_done = sem("ninv_done")
        mchain = sem("mchain")
        mscale_done = sem("mscale_done")
        mT_done = sem("mT_done")
        mhi_done = sem("mhi_done")
        mlo_done = sem("mlo_done")
        stats_done = sem("stats_done")
        mv_done = sem("mv_done")
        ln_chain = sem("ln_chain")
        ln_done = sem("ln_done")
        step_ln_done = sem("step_ln_done")
        xn_done = sem("xn_done")
        xT_done = sem("xT_done")
        xhi_done = sem("xhi_done")
        xlo_done = sem("xlo_done")
        z_done = sem("z_done")
        silu_done = sem("silu_done")
        h_done = sem("h_done")
        hT_done = sem("hT_done")
        hhi_done = sem("hhi_done")
        hlo_done = sem("hlo_done")
        y_done = sem("y_done")
        x1_done = sem("x1_done")
        x2n_done = sem("x2n_done")
        x2T_done = sem("x2T_done")
        x2hi_done = sem("x2hi_done")
        x2lo_done = sem("x2lo_done")
        abs_done = sem("abs_done")
        big_done = sem("big_done")
        sum_done = sem("sum_done")
        q_done = sem("q_done")
        q_used = sem("q_used")
        norm_done = sem("norm_done")
        fchain = sem("fchain")
        b2_done = sem("b2_done")
        pool_f = sem("pool_f")
        binv_done = sem("binv_done")
        fscale_done = sem("fscale_done")
        gate_done = sem("gate_done")
        up_done = sem("up_done")
        sg_done = sem("sg_done")
        fuse_done = sem("fuse_done")
        fh_done = sem("fh_done")
        fl_done = sem("fl_done")
        down_done = sem("down_done")
        acc_done = sem("acc_done")
        acc_free = sem("acc_free")
        added = sem("added")
        added_last = sem("added_last")
        stored = sem("stored")

        N_CONSTS = 15

        def slab_tile(g, t):
            v = X2[:, g, :, :, :, :] if isinstance(g, int) else X2[:, ds(g, 1), :, :, :, :]
            pat = "p a k t i -> p (a k t i)" if isinstance(g, int) else "p g a k t i -> p (g a k t i)"
            return v.rearrange(pat).bitcast(F32)[:, t * D:(t + 1) * D]

        def x2_part(tile, part):
            if isinstance(tile, int):
                return X2[:, tile // TPG, part, :, tile % TPG, :]
            return X2[:, ds(tile >> 2, 1), part, :, ds(tile & 3, 1), :].rearrange("p a k b i -> p (a k b) i")

        def x2_group(g, part, k):
            if isinstance(g, int):
                return X2[:, g, part, k, :, :].rearrange("p t i -> p (t i)")
            return X2[:, ds(g, 1), part, k, :, :].rearrange("p g t i -> p (g t i)")

        def xs_tile(tile):
            if isinstance(tile, int):
                return xs[:, tile, :]
            return xs[:, ds(tile, 1), :].rearrange("p a d -> p (a d)")

        def ln_col(r, which, i):
            if isinstance(r, int):
                return ln_tab[:, r, which, i:i + 1]
            return ln_tab[:, ds(r, 1), which, i:i + 1].rearrange("p a i -> p (a i)")

        block = stack.enter_context(nc.Block())

        @block.sync
        def _(sp):
            sp.dma_start(ids[:], ids_v).then_inc(ids_in, 16)
            sp.dma_start(cs[:, 0], ctx_v[E - 1]).then_inc(ctx_in[0], 16)
            sp.dma_start(gx[:], g_xattn.partition_broadcast(P)).then_inc(params_in, 16)
            sp.dma_start(gf[:], g_ffn.partition_broadcast(P)).then_inc(params_in, 16)
            sp.dma_start(gs_rows[:], gate_scale.rearrange("(c p) -> c p", p=P)).then_inc(params_in, 16)
            sp.dma_start(us_rows[:], up_scale.rearrange("(c p) -> c p", p=P)).then_inc(params_in, 16)
            sp.dma_start(dsc[:], down_scale.partition_broadcast(P)).then_inc(params_in, 16)
            sp.dma_start(cs[:, 1], ctx_v[E - 2]).then_inc(ctx_in[1], 16)

            def load_pair(n):
                if n >= 2:
                    sp.wait_ge(sum_done, n - 1)
                if n < GU_PAIRS:
                    w, m = (gate_v, n) if n < GU_PAIRS // 2 else (up_v, n - GU_PAIRS // 2)
                    a, k = m // 2, 2 * (m % 2)
                    src = w[:, k:k + 2, a * 512:(a + 1) * 512]
                else:
                    d = 2 * (n - GU_PAIRS)
                    src = down_v[:, d:d + 2, :]
                sp.dma_start(ws[:, n % 2], src).then_inc(w_in[n % 2], 16)

            load_pair(0)
            load_pair(1)
            for e in range(2, E):
                sp.wait_ge(mT_done, KC * (e - 1))
                sp.wait_ge(ssq_done, e - 1)
                sp.dma_start(cs[:, e % 2], ctx_v[E - 1 - e]).then_inc(ctx_in[e % 2], 16)
            for n in range(2, PAIRS):
                load_pair(n)

        @block.gpsimd
        def _(pool):
            g = nc.gpsimd
            g.memset(zero[:], 0.0).then_inc(consts, 1)
            g.memset(ones[:], 1.0).then_inc(consts, 1)
            g.memset(mhalf[:], -0.5).then_inc(consts, 1)
            g.memset(ones64[:], 1.0).then_inc(consts, 1)
            g.memset(ln_eps[:], LN_EPS).then_inc(consts, 1)
            g.memset(ln_half[:], -0.5).then_inc(consts, 1)
            g.memset(ln_zero[:], 0.0).then_inc(consts, 1)
            g.iota(iota_q[:], pattern=[[1, P]], base=0, channel_multiplier=0,
                   allow_small_or_imprecise_dtypes=True).then_inc(consts, 1)
            g.iota(tok_no[:], pattern=[[1, TILES]], base=0, channel_multiplier=TILES,
                   allow_small_or_imprecise_dtypes=True).then_inc(consts, 1)
            g.iota(step128[:], pattern=[[P, STEPS]], base=0, channel_multiplier=0,
                   allow_small_or_imprecise_dtypes=True).then_inc(consts, 1)
            g.iota(step_pos[:], pattern=[[P, STEPS]], base=0, channel_multiplier=1,
                   allow_small_or_imprecise_dtypes=True).then_inc(consts, 1)
            g.memset(cge[:, 0], 0.0).then_inc(consts, 1)
            g.memset(cge[:, E], 1.0).then_inc(consts, 1)
            pool.wait_ge(consts, N_CONSTS - 2)
            g.affine_select(out=ident[:], in_=zero[:], compare_op=ALU.not_equal, fill=1.0, base=0,
                            pattern=[[-1, P]], channel_multiplier=1).then_inc(consts, 1)
            g.affine_select(out=below[:], in_=ones[:], compare_op=ALU.is_gt, fill=0.0, base=0,
                            pattern=[[1, P]], channel_multiplier=-1).then_inc(consts, 1)

            pool.wait_ge(tile_eq_done, 1)
            g.tensor_tensor(tile_tok[:], tile_eq[:], tok_no[:].unsqueeze(2).to_broadcast([P, TILES, TILES]),
                            ALU.mult).then_inc(tile_tok_done, 1)

            pool.wait_ge(order_done, 1)

            def gather(t, done):
                g.indirect_dma_start(out=xs[:, t, :], out_offset=None, in_=x_rows[:],
                                     in_offset=bass.IndirectOffsetOnAxis(ap=order[:, t:t + 1], axis=0)
                                     ).then_inc(done, 16)

            def expert_norm(e):
                pool.wait_ge(ssq_done, e + 1)
                g.partition_all_reduce(all_max[:, e:e + 1], part_ssq[:, e:e + 1], P, RMAX).then_inc(pool_m, 1)
                pool.wait_ge(pool_m, 3 * e + 1)
                g.tensor_scalar(n2[:, e:e + 1], all_max[:, e:e + 1], 2.0 ** -40, None, ALU.max).then_inc(pool_m, 1)
                pool.wait_ge(pool_m, 3 * e + 2)
                g.tensor_tensor(n_inv[:, e:e + 1], n2[:, e:e + 1], mhalf[:, 0:1], ALU.pow).then_inc(pool_m, 1)
                pool.wait_ge(pool_m, 3 * e + 3)
                g.tensor_scalar(n_top[:, e:e + 1], n_inv[:, e:e + 1], 2.0 ** 15, None,
                                ALU.mult).then_inc(ninv_done, 1)

            def ln_scalars(batch, r, slot, nr, lo, hi):
                rr = slice(r, r + nr) if isinstance(r, int) else ds(r, nr)
                sl = slice(slot, slot + nr)
                pool.wait_ge(mv_done, batch + 1)
                g.tensor_tensor(var_eps[:, rr, lo:hi], mv[:, sl, lo:hi, 1], ln_eps[:, 0:nr, lo:hi],
                                ALU.add).then_inc(ln_chain, 1)
                pool.wait_ge(ln_chain, 3 * batch + 1)
                g.tensor_tensor(ln_tab[:, rr, lo:hi, 0], var_eps[:, rr, lo:hi], ln_half[:, 0:nr, lo:hi],
                                ALU.pow).then_inc(ln_chain, 1)
                pool.wait_ge(ln_chain, 3 * batch + 2)
                g.tensor_tensor(mean_r[:, rr, lo:hi], mv[:, sl, lo:hi, 0], ln_tab[:, rr, lo:hi, 0],
                                ALU.mult).then_inc(ln_chain, 1)
                pool.wait_ge(ln_chain, 3 * batch + 3)
                g.tensor_tensor(ln_tab[:, rr, lo:hi, 1], ln_zero[:, 0:nr, lo:hi], mean_r[:, rr, lo:hi],
                                ALU.subtract).then_inc(ln_done, 1)

            def step_scalars(s, tile):
                g.tensor_tensor(step_ln[:, ds(s, 1), :], ln_tab[:, ds(tile, 1), 0, :],
                                mask[:, ds(s, 1)].unsqueeze(2).to_broadcast([P, 1, 2]),
                                ALU.mult).then_inc(step_ln_done, 1)

            gather(0, gathered[0])
            expert_norm(0)
            gather(1, gathered[1])
            ln_scalars(0, 0, 0, 1, 0, 1)
            pool.wait_ge(ln_done, 1)
            pool.wait_ge(walk_done, 2)
            step_scalars(0, 0)
            for t in range(2, 8):
                gather(t, gathered[t // 4 + 1])
            ln_scalars(1, 1, 1, 3, 0, 1)
            pool.wait_ge(ln_done, 2)
            expert_norm(1)

            def step(s, lo):
                if lo < STEPS - 1:
                    code = g.value_load(walk[0:1, ds(s, 1)], min_val=0, max_val=4095)
                    if lo >= 1:
                        pool.wait_ge(ln_done, s + 2)
                    step_scalars(s + 1, (code >> 4) & 15)
                if lo < 2:
                    for t in range(8 + 4 * lo, 12 + 4 * lo):
                        gather(t, gathered[t // 4 + 1])
                if lo + 2 < E:
                    expert_norm(lo + 2)
                ln_scalars(s + 2, s + STATS1_LEAD, lo % 2, 1, 0 if lo + STATS1_LEAD < TILES else 1,
                           2 if lo >= STATS2_LAG else 1)
                if lo < PAIRS:
                    pool.wait_ge(big_done, s + 1)
                    g.tensor_tensor(w_sum[:], ws[:, lo % 2], w_big[:, lo % 2], ALU.add).then_inc(sum_done, 1)
                    pool.wait_ge(sum_done, s + 1)
                    g.tensor_tensor(W8[:, ds(2 * s, 2), :], w_sum[:], w_big[:, lo % 2],
                                    ALU.subtract).then_inc(q_done, 1)

            def ffn_norm():
                pool.wait_ge(b2_done, 1)
                g.tensor_tensor(b_inv[:], b2c[:], mhalf[:], ALU.pow).then_inc(pool_f, 1)
                pool.wait_ge(pool_f, 1)
                g.tensor_scalar(f_top[:], b_inv[:], 2.0 ** 15 / 512, None, ALU.mult).then_inc(binv_done, 1)

            for s in range(6):
                step(s, s)
            with pool.Fori(3, 6) as half:
                step(2 * half, 6)
                step(2 * half + 1, 7)
            step(12, 12)
            step(13, 13)
            ffn_norm()
            with pool.Fori(7, 9) as half:
                step(2 * half, 14)
                step(2 * half + 1, 15)
            step(STEPS - 1, STEPS - 1)
            for i in range(2):
                ln_scalars(STEPS + 2 + i, STEPS + STATS1_LEAD + i, 1 - i, 1, 1, 2)

            for t in range(TILES):
                if t < TILES - TPG:
                    pool.wait_ge(acc_free, TPG + t + 1)
                    g.tensor_tensor(xs[:, t, :], xs[:, t, :], slab_tile(t // TPG, t % TPG),
                                    ALU.add).then_inc(added, 1)
                    pool.wait_ge(added, t + 1)
                else:
                    pool.wait_ge(added_last, t - (TILES - TPG) + 1)
                g.indirect_dma_start(out=out_rows[:], out_offset=bass.IndirectOffsetOnAxis(
                    ap=order[:, t:t + 1], axis=0), in_=xs[:, t, :], in_offset=None).then_inc(stored, 16)
            pool.wait_ge(stored, 16 * TILES)

        @block.scalar
        def _(act):
            a = nc.scalar
            def squares(e):
                act.wait_ge(ctx_in[e % 2], 16 * (e // 2 + 1))
                if e:
                    act.wait_ge(ssq_done, e)
                a.activation(junk[:], cs[:, e % 2].rearrange("p r d -> p (r d)"), ACT.Square,
                             accum_out=part_ssq[:, e:e + 1]).then_inc(ssq_done, 1)

            def expert_high(e, chunks, banks):
                act.wait_ge(mscale_done, e + 1)
                for k in chunks:
                    act.wait_ge(mT_done, KC * e + k + 1)
                    a.activation(Mh[:, (e * KC + k) * 512:(e * KC + k + 1) * 512], banks[k % len(banks)][:],
                                 ACT.Identity, scale=m_scale[:, e:e + 1]).then_inc(mhi_done, 1)

            def normalise(s, tile):
                act.wait_ge(step_ln_done, s + 1)
                if isinstance(s, int):
                    mul, add = step_ln[:, s, 0:1], step_ln[:, s, 1:2]
                else:
                    mul, add = (step_ln[:, ds(s, 1), i:i + 1].rearrange("p a i -> p (a i)") for i in range(2))
                a.activation(xn[:], xs_tile(tile), ACT.Identity, scale=mul, bias=add).then_inc(xn_done, 1)

            def x_high(s):
                act.wait_ge(xT_done, s + 1)
                a.activation(xTh[:], XT[:], ACT.Copy, scale=X_SCALE).then_inc(xhi_done, 1)

            def normalise2(tile):
                act.wait_ge(ln_done, tile + 8)
                if not (isinstance(tile, int) and tile == 0):
                    act.wait_ge(x2T_done, tile)
                r = tile + STATS1_LEAD + STATS2_LAG
                a.activation(x2n[:], xs_tile(tile), ACT.Identity, scale=ln_col(r, 1, 0),
                             bias=ln_col(r, 1, 1)).then_inc(x2n_done, 1)

            def x2_high(tile, src):
                act.wait_ge(x2T_done, tile + 1)
                a.activation(x2_part(tile, 0), src[:].rearrange("p (k i) -> p k i", k=KC),
                             ACT.Copy, scale=X_SCALE).then_inc(x2hi_done, 1)

            def scale_down(n):
                act.wait_ge(q_done, n + 1)
                for i in range(2):
                    w = W8[:, ds(2 * n + i, 1), :].rearrange("p a n -> p (a n)")
                    ins = a.activation(w, w, ACT.Copy, scale=f_inv[:, ds(2 * (n - GU_PAIRS) + i, 1)])
                ins.then_inc(q_used, 1)

            squares(0)
            act.wait_ge(params_in, 80)
            a.activation(tgx[:], gx[:], ACT.Tanh).then_inc(tanh_done, 1)
            a.activation(tgf[:], gf[:], ACT.Tanh).then_inc(tanh_done, 1)
            a.activation(warm[:], gx[:], ACT.Silu)
            expert_high(0, range(KC), MT_FIRST)
            normalise(0, 0)
            squares(1)
            x_high(0)

            def step(s, lo):
                prev, nxt = lo >= 1, lo < STEPS - 1
                code = a.value_load(walk[0:1, ds(s, 1)], min_val=0, max_val=4095)
                e = code & 3
                if prev:
                    act.wait_ge(hT_done, s)
                    if lo >= 2:
                        act.wait_ge(y_done, s - 1)
                    a.activation(hTh[:], HT[:], ACT.Copy).then_inc(hhi_done, 1)
                if nxt:
                    act.wait_ge(xT_done, s + 1)
                    if lo >= 2:
                        act.wait_ge(x1_done, s - 1)
                    if lo == 0:
                        act.wait_ge(gathered[1], 48)
                    normalise(s + 1, (code >> 4) & 15)
                if lo < PAIRS:
                    act.wait_ge(w_in[lo % 2], 8 * (s - lo % 2) + 16)
                    if lo >= 2:
                        act.wait_ge(q_done, s - 1)
                    a.activation(w_big[:, lo % 2], ws[:, lo % 2], ACT.Abs, scale=FP8_STEP).then_inc(abs_done, 1)
                if lo >= X2_LAG:
                    normalise2(s - X2_LAG)
                if lo + 1 < E:
                    expert_high(lo + 1, (0, 1), MT)
                act.wait_ge(z_done, s + 1)
                if prev:
                    act.wait_ge(h_done, s)
                a.activation(silu_z[:], Z[:], ACT.Silu, scale=z_scale[:, ds(e, 1)]).then_inc(silu_done, 1)
                if lo + 1 < E:
                    expert_high(lo + 1, (2, 3), MT)
                if nxt:
                    x_high(s + 1)
                if lo >= X2_LAG:
                    x2_high(s - X2_LAG, X2T)
                if NORM_LAG <= lo < GU_PAIRS + NORM_LAG:
                    act.wait_ge(q_done, s - 1)
                    if lo > NORM_LAG:
                        act.wait_ge(norm_done, s - NORM_LAG)
                    a.activation(sq[:], W8[:, ds(2 * (s - NORM_LAG), 2), :], ACT.Square).then_inc(q_used, 1)
                elif lo >= GU_PAIRS + NORM_LAG:
                    act.wait_ge(fscale_done, 1)
                    scale_down(s - NORM_LAG)
                if lo + 2 < E:
                    squares(lo + 2)

            for s in range(6):
                step(s, s)
            with act.Fori(3, 6) as half:
                step(2 * half, 6)
                step(2 * half + 1, 7)
            step(12, 12)
            step(13, 13)
            with act.Fori(7, 9) as half:
                step(2 * half, 14)
                step(2 * half + 1, 15)
            step(STEPS - 1, STEPS - 1)

            def last_h_high():
                act.wait_ge(hT_done, STEPS)
                act.wait_ge(y_done, STEPS - 1)
                a.activation(hTh[:], HT[:], ACT.Copy).then_inc(hhi_done, 1)

            def gate_silu(g, c):
                act.wait_ge(gate_done, g * IC + c + 1)
                if not (isinstance(g, int) and g * IC + c < 2):
                    act.wait_ge(fuse_done, g * IC + c - 1)
                a.activation(sg[:, c % 2, :], GATE[c % 2][:], ACT.Silu,
                             scale=gate_mul[:, c:c + 1]).then_inc(sg_done, 1)

            def fuse_high(g, c):
                act.wait_ge(fuse_done, g * IC + c + 1)
                if not (isinstance(g, int) and g * IC + c < 2):
                    act.wait_ge(down_done, g * IC + c - 1)
                a.activation(fh[:, c % 2, :], fuse[:, c % 2, :], ACT.Copy).then_inc(fh_done, 1)

            last_h_high()
            normalise2(TILES - 3)
            x2_high(TILES - 3, XT)
            scale_down(PAIRS - 1)
            normalise2(TILES - 2)
            x2_high(TILES - 2, XT)
            gate_silu(0, 0)
            normalise2(TILES - 1)
            fuse_high(0, 0)
            x2_high(TILES - 1, XT)
            gate_silu(0, 1)
            fuse_high(0, 1)

            def group(g, last):
                for c in range(2, IC):
                    gate_silu(g, c)
                    fuse_high(g, c)
                if not last:
                    for c in range(2):
                        gate_silu(g + 1, c)
                        fuse_high(g + 1, c)

            with act.Fori(0, GROUPS - 1) as gi:
                group(gi, False)
            group(GROUPS - 1, True)

        @block.vector
        def _(dve):
            v = nc.vector
            chained = [0]

            def link(ins, s_, count):
                count[0] += 1
                ins.then_inc(s_, 1)
                dve.wait_ge(s_, count[0])

            dve.wait_ge(ids_in, 16)
            dve.wait_ge(consts, N_CONSTS)
            link(v.tensor_copy(idf[:], ids[:]), sort_v, chained)
            for j in range(1, E):
                ins = v.tensor_scalar(cge[:, j], idf[:], float((E - j) * PER_EXPERT), None, ALU.is_ge)
            link(ins, sort_v, chained)
            v.tensor_tensor(onehot[:], cge[:, 1:E + 1, :].rearrange("p e c -> p (e c)"),
                            cge[:, 0:E, :].rearrange("p e c -> p (e c)"), ALU.subtract).then_inc(onehot_done, 1)
            dve.wait_ge(counts_done, 1)
            link(v.tensor_copy(total[:], SMALL[:, 64:128]), sort_v, chained)
            link(v.tensor_tensor_scan(incl[:], ones64[:], total[:], 0.0, ALU.mult, ALU.add), sort_v, chained)
            link(v.tensor_tensor(base[:], incl[:], total[:], ALU.subtract), sort_v, chained)
            link(v.tensor_tensor(rank_e[:], SMALL[:, 0:64], base[:], ALU.add), sort_v, chained)
            link(v.tensor_tensor(rank_m[:], rank_e[:], onehot[:], ALU.mult), sort_v, chained)
            link(v.tensor_reduce(rank[:], rank_m[:].rearrange("p (e c) -> p c e", e=E), AX.X, ALU.add),
                 sort_v, chained)
            link(v.tensor_copy(rank_i[:], rank[:]), sort_v, chained)
            v.tensor_scalar(tile_i[:], rank_i[:], 7, None, ALU.arith_shift_right)
            link(v.tensor_scalar(row_i[:], rank_i[:], P - 1, None, ALU.bitwise_and), sort_v, chained)
            v.tensor_copy(row_f[:], row_i[:])
            v.tensor_copy(tile_f[:], tile_i[:]).then_inc(place_done, 1)
            dve.wait_ge(place_done, 1)
            v.tensor_tensor(tile_eq[:], iota_q[:, 0:TILES].unsqueeze(1).to_broadcast([P, TILES, TILES]),
                            tile_f[:].unsqueeze(2).to_broadcast([P, TILES, TILES]),
                            ALU.is_equal).then_inc(tile_eq_done, 1)
            v.tensor_tensor(row_hot[:], iota_q[:].unsqueeze(1).to_broadcast([P, TILES, P]),
                            row_f[:].unsqueeze(2).to_broadcast([P, TILES, P]), ALU.is_equal).then_inc(row_hot_done, 1)
            dve.wait_ge(order_mm, 1)
            v.tensor_copy(order[:], SMALL[:, 128:128 + TILES]).then_inc(order_done, 1)

            starts = [base[:, e * TILES:e * TILES + 1] for e in range(1, E)]
            for e in range(1, E):
                ins = v.tensor_scalar(bound[:, e - 1:e], starts[e - 1], float(TOK - 1), None, ALU.min)
            link(ins, sort_v, chained)
            for e in range(1, E):
                ins = v.tensor_scalar(past[:, e - 1], step128[:], float(P - P * e), bound[:, e - 1:e],
                                      ALU.add, ALU.is_gt)
            link(ins, sort_v, chained)
            link(v.tensor_tensor(past2[:], past[:, 0], past[:, 1], ALU.add), sort_v, chained)
            link(v.tensor_tensor(e_of[:], past2[:], past[:, 2], ALU.add), sort_v, chained)
            v.scalar_tensor_tensor(out=pos[:], in0=e_of[:], scalar=-float(P), in1=step_pos[:],
                                   op0=ALU.mult, op1=ALU.add)
            v.tensor_copy(walk_f[:], e_of[:])
            link(v.scalar_tensor_tensor(out=tile_of[:], in0=step128[:], scalar=1.0 / P, in1=e_of[:],
                                        op0=ALU.mult, op1=ALU.subtract), sort_v, chained)
            link(v.scalar_tensor_tensor(out=walk_f[:, 1:], in0=e_of[:, :-1], scalar=4.0, in1=walk_f[:, 1:],
                                        op0=ALU.mult, op1=ALU.add), sort_v, chained)
            link(v.scalar_tensor_tensor(out=walk_f[:, :-1], in0=tile_of[:, 1:], scalar=16.0, in1=walk_f[:, :-1],
                                        op0=ALU.mult, op1=ALU.add), sort_v, chained)
            link(v.scalar_tensor_tensor(out=walk_f[:, 1:], in0=tile_of[:, :-1], scalar=256.0, in1=walk_f[:, 1:],
                                        op0=ALU.mult, op1=ALU.add), sort_v, chained)
            v.tensor_scalar(last_f[:], tile_of[:, STEPS - 1:STEPS], 64.0, e_of[:, STEPS - 1:STEPS], ALU.mult, ALU.add)
            link(v.tensor_copy(walk[:], walk_f[:]), sort_v, chained)
            v.tensor_scalar(walk_last[:], last_f[:], 4.0, None, ALU.mult).then_inc(walk_done, 1)
            for e in range(1, E):
                ins = v.tensor_scalar(cnt[:, e - 1], pos[:], starts[e - 1], None, ALU.is_ge)
            link(ins, sort_v, chained)
            link(v.tensor_tensor(cnt2[:], cnt[:, 0], cnt[:, 1], ALU.add), sort_v, chained)
            link(v.tensor_tensor(cnt3[:], cnt2[:], cnt[:, 2], ALU.add), sort_v, chained)
            v.tensor_tensor(mask[:], cnt3[:], e_of[:], ALU.is_equal).then_inc(walk_done, 1)

            dve.wait_ge(tanh_done, 2)
            v.tensor_scalar(tgx24[:], tgx[:], 2.0 ** 24, None, ALU.mult).then_inc(gates_done, 1)
            v.tensor_scalar(dsb[:], dsc[:], tgf[:, 0:1], None, ALU.mult).then_inc(gates_done, 1)
            dve.wait_ge(gates_done, 2)

            dve.wait_ge(scales_T, 1)
            v.tensor_copy(gs[:], SMALL[:, 160:160 + IC])
            v.tensor_copy(us[:], SMALL[:, 176:176 + IC]).then_inc(scales_done, 1)

            mcount = [0]

            def expert_scale(e):
                c = slice(e, e + 1)
                dve.wait_ge(ninv_done, e + 1)
                link(v.tensor_scalar(m_scale[:, c].bitcast(I32), n_top[:, c].bitcast(I32), POW2_MASK, None,
                                     ALU.bitwise_and), mchain, mcount)
                link(v.reciprocal(m_inv[:, c], m_scale[:, c]), mchain, mcount)
                v.tensor_scalar(z_scale[:, c], m_inv[:, c], 1.0 / X_SCALE, None, ALU.mult)
                v.tensor_scalar(h_scale[:, c], m_scale[:, c], 2.0 ** -24 / X_SCALE, None, ALU.mult)
                link(v.tensor_tensor(m_inv2[:, c], m_inv[:, c], m_inv[:, c], ALU.mult), mchain, mcount)
                v.scalar_tensor_tensor(out=y_scale[:, c], in0=m_inv2[:, c], scalar=tgx24[:, 0:1], in1=m_inv[:, c],
                                       op0=ALU.mult, op1=ALU.mult).then_inc(mscale_done, 1)

            def expert_low(e, chunks, banks):
                dve.wait_ge(mscale_done, e + 1)
                for k in chunks:
                    w = slice((e * KC + k) * 512, (e * KC + k + 1) * 512)
                    dve.wait_ge(mhi_done, KC * e + k + 1)
                    v.scalar_tensor_tensor(out=Ml[:, w], in0=banks[k % len(banks)][:], scalar=m_scale[:, e:e + 1],
                                           in1=Mh[:, w], op0=ALU.mult, op1=ALU.subtract).then_inc(mlo_done, 1)

            def tile_stats(slot, which, tile):
                return v.bn_stats(stats[:, slot, which, :], xs_tile(tile))

            def aggregate(batch, slots, lo, hi):
                dve.wait_ge(stats_done, batch + 1)
                if not (isinstance(batch, int) and batch < 2):
                    dve.wait_ge(ln_done, batch - 1)
                dve.nop(nofuse=True)
                for slot in slots:
                    for i in range(lo, hi):
                        ins = v.bn_aggr(mv[:, slot, i, :], stats[:, slot, i, :])
                ins.then_inc(mv_done, 1)

            def x_low(dst, src, high, ready, n):
                dve.wait_ge(ready, n)
                return v.scalar_tensor_tensor(out=dst, in0=src, scalar=X_SCALE, in1=high, op0=ALU.mult,
                                              op1=ALU.subtract)

            def x2_low(tile, src):
                return x_low(x2_part(tile, 1), src[:].rearrange("p (k i) -> p k i", k=KC), x2_part(tile, 0),
                             x2hi_done, tile + 1)

            def h_low(s, lo):
                dve.wait_ge(hhi_done, s + 1)
                if lo >= 1:
                    dve.wait_ge(y_done, s)
                v.tensor_tensor(hTl[:], HT[:], hTh[:], ALU.subtract).then_inc(hlo_done, 1)

            dve.wait_ge(gathered[0], 16)
            tile_stats(0, 0, 0).then_inc(stats_done, 1)
            aggregate(0, [0], 0, 1)
            expert_scale(0)
            expert_low(0, range(KC), MT_FIRST)
            x_low(xTl[:], XT[:], xTh[:], xhi_done, 1).then_inc(xlo_done, 1)
            dve.wait_ge(gathered[1], 48)
            for t in range(1, 4):
                ins = tile_stats(t, 0, t)
            ins.then_inc(stats_done, 1)
            aggregate(1, [1, 2, 3], 0, 1)

            def add_expert(s, code, xn_reads):
                dve.wait_ge(y_done, s + 1)
                if xn_reads is not None:
                    dve.wait_ge(xn_done, xn_reads)
                row = xs_tile((code >> 8) & 15)
                v.scalar_tensor_tensor(out=row, in0=Y[:], scalar=y_scale[:, ds((code >> 2) & 3, 1)], in1=row,
                                       op0=ALU.mult, op1=ALU.add).then_inc(x1_done, 1)

            def step(s, lo):
                prev, nxt = lo >= 1, lo < STEPS - 1
                code = v.value_load(walk[0:1, ds(s, 1)], min_val=0, max_val=4095)
                if prev:
                    h_low(s - 1, lo - 1)
                if lo == 0:
                    dve.wait_ge(gathered[2], 64)
                if lo == 4:
                    dve.wait_ge(gathered[3], 64)
                    dve.wait_ge(gathered[4], 64)
                first, last = (0 if lo + STATS1_LEAD < TILES else 1), (2 if lo >= STATS2_LAG else 1)
                slot = lo % 2
                if first == 0:
                    ins = tile_stats(slot, 0, s + STATS1_LEAD)
                if last == 2:
                    dve.wait_ge(x1_done, s - 1)
                    ins = tile_stats(slot, 1, s - STATS2_LAG)
                ins.then_inc(stats_done, 1)
                aggregate(s + 2, [slot], first, last)
                if lo < PAIRS:
                    dve.wait_ge(abs_done, s + 1)
                    v.tensor_scalar(w_big[:, lo % 2], w_big[:, lo % 2], FP8_FLOOR, None,
                                    ALU.max).then_inc(big_done, 1)
                if lo + 1 < E:
                    expert_scale(lo + 1)
                    expert_low(lo + 1, (0, 1), MT)
                dve.wait_ge(silu_done, s + 1)
                if prev:
                    dve.wait_ge(hT_done, s)
                v.scalar_tensor_tensor(out=h[:], in0=Z[:], scalar=h_scale[:, ds(code & 3, 1)], in1=silu_z[:],
                                       op0=ALU.mult, op1=ALU.mult).then_inc(h_done, 1)
                if lo + 1 < E:
                    expert_low(lo + 1, (2, 3), MT)
                if nxt:
                    x_low(xTl[:], XT[:], xTh[:], xhi_done, s + 2).then_inc(xlo_done, 1)
                if lo >= X2_LAG:
                    x2_low(s - X2_LAG, X2T).then_inc(x2lo_done, 1)
                if prev:
                    add_expert(s - 1, code, s + 2 if nxt else None)

            for s in range(6):
                step(s, s)
            with dve.Fori(3, 6) as half:
                step(2 * half, 6)
                step(2 * half + 1, 7)
            step(12, 12)
            step(13, 13)

            fcount = [0]
            dve.wait_ge(scales_done, 1)
            dve.wait_ge(norm_done, GU_PAIRS)
            norms = SMALL[:, 0:2 * THIRDS * KC * KC].rearrange("p (m k j) -> p m j k", k=KC, j=KC)
            link(v.tensor_reduce(col_ssq[:].rearrange("p w (a j) -> p (w a) j", j=KC), norms, AX.X, ALU.add),
                 fchain, fcount)
            v.tensor_tensor(nn[:], col_ssq[:, 0, :], col_ssq[:, 1, :], ALU.mult)
            link(v.tensor_tensor(gu[:], gs[:], us[:], ALU.mult), fchain, fcount)
            link(v.tensor_tensor(gu2[:], gu[:], gu[:], ALU.mult), fchain, fcount)
            link(v.tensor_tensor(b2[:], nn[:], gu2[:], ALU.mult), fchain, fcount)
            v.tensor_scalar(b2c[:], b2[:], 1e-30, 1e38, ALU.max, ALU.min).then_inc(b2_done, 1)
            dve.wait_ge(binv_done, 1)
            link(v.tensor_scalar(f_scale[:].bitcast(I32), f_top[:].bitcast(I32), POW2_MASK, None,
                                 ALU.bitwise_and), fchain, fcount)
            v.tensor_scalar(gate_mul[:], gs[:], 1.0 / X_SCALE, None, ALU.mult)
            link(v.tensor_scalar(up_mul0[:], us[:], 1.0 / X_SCALE, None, ALU.mult), fchain, fcount)
            v.tensor_tensor(up_mul[:], up_mul0[:], f_scale[:], ALU.mult)
            v.reciprocal(f_inv[:], f_scale[:]).then_inc(fscale_done, 1)

            with dve.Fori(7, 9) as half:
                step(2 * half, 14)
                step(2 * half + 1, 15)
            step(STEPS - 1, STEPS - 1)

            h_low(STEPS - 1, STEPS - 1)
            dve.wait_ge(x1_done, STEPS - 1)
            tile_stats(1, 1, TILES - 2).then_inc(stats_done, 1)
            aggregate(STEPS + 2, [1], 1, 2)
            x2_low(TILES - 3, XT).then_inc(x2lo_done, 1)
            last = v.value_load(walk_last[0:1, 0:1], min_val=0, max_val=4095)
            add_expert(STEPS - 1, last, None)
            dve.wait_ge(x1_done, STEPS)
            tile_stats(0, 1, TILES - 1).then_inc(stats_done, 1)
            aggregate(STEPS + 3, [0], 1, 2)
            x2_low(TILES - 2, XT).then_inc(x2lo_done, 1)

            def ffn_unit(g, c):
                u = g * IC + c
                dve.wait_ge(up_done, u + 1)
                dve.wait_ge(sg_done, u + 1)
                if not (isinstance(g, int) and g * IC + c < 2):
                    dve.wait_ge(fl_done, u - 1)
                v.scalar_tensor_tensor(out=fuse[:, c % 2, :], in0=UP[c % 2][:], scalar=up_mul[:, c:c + 1],
                                       in1=sg[:, c % 2, :], op0=ALU.mult, op1=ALU.mult).then_inc(fuse_done, 1)
                if not (isinstance(g, int) and g * IC + c < 2):
                    dve.wait_ge(down_done, u - 1)
                dve.wait_ge(fh_done, u + 1)
                v.tensor_tensor(fl[:, c % 2, :], fuse[:, c % 2, :], fh[:, c % 2, :],
                                ALU.subtract).then_inc(fl_done, 1)

            ffn_unit(0, 0)
            x2_low(TILES - 1, XT).then_inc(acc_free, TPG)

            ffn_unit(0, 1)

            def group(g, last):
                for c in range(2, IC):
                    ffn_unit(g, c)
                if not last:
                    ffn_unit(g + 1, 0)
                for t in range(TPG):
                    if t < TPG - 1:
                        dve.wait_ge(acc_done, g * (TPG - 1) + t + 1)
                    else:
                        dve.wait_ge(down_done, g * IC + IC)
                    v.tensor_tensor(slab_tile(g, t), ACC[t][:], dsb[:], ALU.mult).then_inc(acc_free, 1)
                    if last:
                        dve.wait_ge(acc_free, TPG + g * TPG + t + 1)
                        v.tensor_tensor(xs[:, g * TPG + t, :], xs[:, g * TPG + t, :], slab_tile(g, t),
                                        ALU.add).then_inc(added_last, 1)
                if not last:
                    ffn_unit(g + 1, 1)

            with dve.Fori(0, GROUPS - 1) as gi:
                group(gi, False)
            group(GROUPS - 1, True)

        @block.tensor
        def _(pe):
            t_ = nc.tensor

            def transpose4(dst, src, done):
                for k in range(KC):
                    ins = t_.matmul(dst[:, k * P:(k + 1) * P], src[:, k * P:(k + 1) * P], ident[:],
                                    is_transpose=True, start=(k == 0), stop=(k == KC - 1))
                ins.then_inc(done, 1)

            pe.wait_ge(consts, N_CONSTS)
            pe.wait_ge(onehot_done, 1)
            t_.matmul(SMALL[:, 0:64], below[:], onehot[:], start=True, stop=True)
            t_.matmul(SMALL[:, 64:128], ones[:], onehot[:], start=True, stop=True).then_inc(counts_done, 1)

            def expert_turn(e, chunks, banks):
                pe.wait_ge(ctx_in[e % 2], 16 * (e // 2 + 1))
                for k in chunks:
                    if e:
                        pe.wait_ge(mlo_done, KC * e + max(k - 1, 0))
                    for r in range(KC):
                        ins = t_.matmul(banks[k % len(banks)][:, r * P:(r + 1) * P], cs[:, e % 2, r, k * P:(k + 1) * P],
                                        ident[:], is_transpose=True, start=(r == 0), stop=(r == KC - 1))
                    ins.then_inc(mT_done, 1)

            pe.wait_ge(row_hot_done, 1)
            pe.wait_ge(tile_tok_done, 1)
            for c in range(TILES):
                ins = t_.matmul(SMALL[:, 128:128 + TILES], row_hot[:, c, :], tile_tok[:, c, :],
                                start=(c == 0), stop=(c == TILES - 1))
            ins.then_inc(order_mm, 1)
            pe.wait_ge(params_in, 80)
            pe.wait_ge(order_done, 1)
            t_.matmul(SMALL[:, 160:160 + IC], gs_rows[:], ident[0:IC, 0:IC], is_transpose=True, start=True, stop=True)
            t_.matmul(SMALL[:, 176:176 + IC], us_rows[:], ident[0:IC, 0:IC], is_transpose=True, start=True,
                      stop=True).then_inc(scales_T, 1)
            expert_turn(0, range(KC), MT_FIRST)
            pe.wait_ge(xn_done, 1)
            transpose4(XT, xn, xT_done)
            pe.wait_ge(walk_done, 2)

            def product(dst, e, high, low, done):
                n = 0
                for k in range(KC):
                    mh = Mh[:, ds(e * (KC * 512) + k * 512, 512)]
                    ml = Ml[:, ds(e * (KC * 512) + k * 512, 512)]
                    for lhs, rhs in ((high, mh), (high, ml), (low, mh)):
                        ins = t_.matmul(dst[:], lhs[:, k * P:(k + 1) * P], rhs, start=(n == 0), stop=(n == 3 * KC - 1))
                        n += 1
                ins.then_inc(done, 1)

            def turn_h(s):
                pe.wait_ge(h_done, s + 1)
                transpose4(HT, h, hT_done)

            def turn_x2(tile, dst):
                pe.wait_ge(x2n_done, tile + 1)
                if not (isinstance(tile, int) and tile == 0):
                    pe.wait_ge(x2lo_done, tile)
                transpose4(dst, x2n, x2T_done)

            def product_y(s, e):
                pe.wait_ge(hlo_done, s + 1)
                if not (isinstance(s, int) and s == 0):
                    pe.wait_ge(x1_done, s)
                product(Y, e, hTh, hTl, y_done)

            def step(s, lo):
                code = t_.value_load(walk[0:1, ds(s, 1)], min_val=0, max_val=4095)
                if lo >= 1:
                    if lo >= 2:
                        pe.wait_ge(hlo_done, s - 1)
                    turn_h(s - 1)
                if lo + 1 < E:
                    expert_turn(lo + 1, (0, 1), MT)
                pe.wait_ge(xlo_done, s + 1)
                pe.wait_ge(mlo_done, KC * (min(lo, E - 1) + 1))
                product(Z, code & 3, xTh, xTl, z_done)
                if lo + 1 < E:
                    expert_turn(lo + 1, (2, 3), MT)
                if lo < STEPS - 1:
                    pe.wait_ge(xn_done, s + 2)
                    transpose4(XT, xn, xT_done)
                if lo >= X2_LAG:
                    turn_x2(s - X2_LAG, X2T)
                if lo >= 1:
                    product_y(s - 1, (code >> 2) & 3)
                if NORM_LAG <= lo < GU_PAIRS + NORM_LAG:
                    norms(s - NORM_LAG)

            def norms(n):
                pe.wait_ge(q_used, n + 1)
                if isinstance(n, int) and n == 0:
                    pe.wait_ge(scales_done, 1)
                for i in range(2):
                    for j in range(KC):
                        ins = t_.matmul(SMALL[:, ds(2 * KC * n + i * KC + j, 1)], sq[:, i, j * P:(j + 1) * P],
                                        ones[:, 0:1], start=True, stop=True)
                ins.then_inc(norm_done, 1)

            for s in range(6):
                step(s, s)
            with pe.Fori(3, 6) as half:
                step(2 * half, 6)
                step(2 * half + 1, 7)
            step(12, 12)
            step(13, 13)
            with pe.Fori(7, 9) as half:
                step(2 * half, 14)
                step(2 * half + 1, 15)
            step(STEPS - 1, STEPS - 1)

            def gate_up(g, c):
                a, j = c // KC, c % KC
                for dst, first, free, done in ((GATE, 0, sg_done, gate_done), (UP, IC, fuse_done, up_done)):
                    if not (isinstance(g, int) and g * IC + c < 2):
                        pe.wait_ge(free, g * IC + c - 1)
                    for k in range(KC):
                        w = W8[:, first + a * KC + k, j * P:(j + 1) * P]
                        for part in range(2):
                            ins = t_.matmul(dst[c % 2][:], w, x2_group(g, part, k), start=(k == 0 and part == 0),
                                            stop=(k == KC - 1 and part == 1))
                    ins.then_inc(done, 1)

            def down(g, c):
                pe.wait_ge(fl_done, g * IC + c + 1)
                for t in range(TPG):
                    if c == 0:
                        pe.wait_ge(acc_free, g * TPG + t + 1)
                    for part in (fh, fl):
                        ins = t_.matmul(ACC[t][:], part[:, c % 2, t * P:(t + 1) * P], W8[:, 2 * IC + c, :],
                                        start=(c == 0 and part is fh), stop=(c == IC - 1 and part is fl))
                    if c == IC - 1 and t < TPG - 1:
                        ins.then_inc(acc_done, 1)
                ins.then_inc(down_done, 1)

            code = t_.value_load(walk_last[0:1, 0:1], min_val=0, max_val=4095)
            pe.wait_ge(hlo_done, STEPS - 1)
            turn_h(STEPS - 1)
            pe.wait_ge(fscale_done, 1)
            pe.wait_ge(xlo_done, STEPS)
            turn_x2(TILES - 3, XT)
            gate_up(0, 0)
            product_y(STEPS - 1, (code >> 2) & 3)
            turn_x2(TILES - 2, XT)
            gate_up(0, 1)
            turn_x2(TILES - 1, XT)
            pe.wait_ge(q_used, PAIRS)
            down(0, 0)

            def group(g, last):
                for c in range(2, IC):
                    gate_up(g, c)
                    down(g, c - 1)
                if not last:
                    gate_up(g + 1, 0)
                down(g, IC - 1)
                if not last:
                    gate_up(g + 1, 1)
                    down(g + 1, 0)

            with pe.Fori(0, GROUPS - 1) as gi:
                group(gi, False)
            group(GROUPS - 1, True)


_INS = ["x", "itok_BxS_13_99985", "ctx_2048", "g_xattn", "g_ffn", "L0_ffn_gate_w", "L0_ffn_up_w", "L0_ffn_down_w",
        "L0_ffn_gate_scale", "L0_ffn_up_scale", "L0_ffn_down_scale"]


def kernel(**inputs):
    import numpy as np
    import concourse.bacc as bacc
    from concourse.bass_utils import run_bass_kernel_spmd as run

    nc = bacc.Bacc("TRN2", target_bir_lowering=False, num_devices=1)
    arrays, args = {}, []
    for name in _INS:
        a = np.ascontiguousarray(inputs[name])
        arrays["in_" + name] = a
        args.append(nc.dram_tensor("in_" + name, a.shape, mybir.dt.from_np(a.dtype), kind="ExternalInput").ap())
    args.append(nc.dram_tensor("out_0", inputs["x"].shape, mybir.dt.float32, kind="ExternalOutput").ap())
    build(nc, *args)
    r = run(nc, [arrays], core_ids=[0])
    return r.results[0]["out_0"]
```

```python
from contextlib import ExitStack

import concourse.bass as bass
from concourse import mybir

F32, F16, BF16, I32 = mybir.dt.float32, mybir.dt.float16, mybir.dt.bfloat16, mybir.dt.int32
ALU = mybir.AluOpType
ACT = mybir.ActivationFunctionType
AX = mybir.AxisListType
RMAX = bass.bass_isa.ReduceOp.max
ds = bass.ds

P = 128
LN_EPS = 1e-5
VOCAB, EXPERTS = 25000, 4
PER_EXPERT = VOCAB // EXPERTS
X_SCALE = 2.0 ** 11
POW2_MASK = 0x7F800000
FP8_STEP = 2.0 ** 20
FP8_FLOOR = FP8_STEP * 2.0 ** -6 * (1 + 2.0 ** -19)


def build(nc, x, token_ids, ctx, g_xattn, g_ffn, gate_w, up_w, down_w, gate_scale, up_scale, down_scale, out):
    B, S, D = x.shape
    TOK = B * S
    TILES = TOK // P
    E = ctx.shape[0]
    KC = D // P
    INNER = gate_w.shape[1]
    IC = INNER // P
    STEPS = TILES + E - 1
    GROUPS = TOK // 512
    TPG = TILES // GROUPS
    SLABS = 3 * IC
    EARLY = 22
    EARLY_NORMS = 18
    MORE_GU = 26
    LAST_DOWN = 32
    STATS1_LEAD = 4
    BATCH_LEAD = 3
    STATS2_LAG = 5
    X2_LAG = 6
    ROUNDS = TILES + STATS1_LEAD + STATS2_LAG
    assert E == EXPERTS and KC == 4 and D == 512 and IC == 3 * KC

    x_rows = x.rearrange("b s d -> (b s) d")
    out_rows = out.rearrange("b s d -> (b s) d")
    ids_v = token_ids.rearrange("b s -> (b s)").rearrange("(p c) -> p c", c=TILES)
    ctx_v = ctx.rearrange("e (r p) d -> e p r d", p=P)
    gate_v = gate_w.rearrange("(k p) n -> p k n", p=P)
    up_v = up_w.rearrange("(k p) n -> p k n", p=P)
    down_v = down_w.rearrange("(k p) n -> p k n", p=P)

    with ExitStack() as stack:
        def sb(name, shape, dt):
            return stack.enter_context(nc.sbuf_tensor(name, shape, dt))

        def sem(name):
            return stack.enter_context(nc.semaphore(name))

        xs = sb("xs", [P, TILES, D], F32)
        Mh = sb("Mh", [P, E * KC * 512], F16)
        Ml = sb("Ml", [P, E * KC * 512], F16)
        X2 = sb("X2", [P, GROUPS, 2, KC, TPG, P], F16)
        W8 = sb("W8", [P, 3 * IC, 512], BF16)
        cs = sb("cs", [P, 2, KC, D], F32)
        ws = sb("ws", [P, 4, 512], F32)
        w_big = sb("w_big", [P, 4, 512], F32)
        w_sum = sb("w_sum", [P, 512], F32)
        sq = sb("sq", [P, 2, 512], BF16)
        junk = sb("junk", [P, KC * D], BF16)
        warm = sb("warm", [P, 1], F32)
        xn = sb("xn", [P, D], F32)
        x2n = sb("x2n", [P, D], F32)
        xTh = sb("xTh", [P, KC * P], F16)
        xTl = sb("xTl", [P, KC * P], F16)
        hTh = sb("hTh", [P, KC * P], F16)
        hTl = sb("hTl", [P, KC * P], F16)
        silu_z = sb("silu_z", [P, 512], F32)
        h = sb("h", [P, 512], F32)
        sg = cs[:, 0, 0:2, :]
        fuse = cs[:, 0, 2:4, :]
        fh = cs[:, 1, 0:1, :].rearrange("p a n -> p (a n)").bitcast(F16).rearrange("p (b n) -> p b n", b=2)
        fl = cs[:, 1, 1:2, :].rearrange("p a n -> p (a n)").bitcast(F16).rearrange("p (b n) -> p b n", b=2)
        ident = sb("ident", [P, P], F32)
        zero = sb("zero", [P, P], F32)
        below = sb("below", [P, P], BF16)
        ones = sb("ones", [P, P], BF16)
        ones32 = sb("ones32", [P, P], F32)
        iota_q = sb("iota_q", [P, P], F16)
        tok_no = sb("tok_no", [P, TILES], F16)
        step128 = sb("step128", [P, STEPS], F32)
        step_pos = sb("step_pos", [P, STEPS], F32)
        ones64 = sb("ones64", [P, E * TILES], F32)
        ln_half = sb("ln_half", [P, 3, 2], F32)
        mhalf = sb("mhalf", [P, IC], F32)
        ids = sb("ids", [P, TILES], I32)
        cge = sb("cge", [P, E + 1, TILES], F32)
        onehot = sb("onehot", [P, E * TILES], BF16)
        incl = sb("incl", [P, E * TILES], F32)
        base = sb("base", [P, E * TILES], F32)
        rank_e = sb("rank_e", [P, E * TILES], F32)
        rank_m = sb("rank_m", [P, E * TILES], F32)
        rank_f = sb("rank_f", [P, TILES], F32)
        rank_i = sb("rank_i", [P, TILES], I32)
        row_i = sb("row_i", [P, TILES], I32)
        tile_i = sb("tile_i", [P, TILES], I32)
        row_f = sb("row_f", [P, TILES], F32)
        tile_f = sb("tile_f", [P, TILES], F16)
        row_hot = sb("row_hot", [P, TILES, P], F16)
        tile_eq = sb("tile_eq", [P, TILES, TILES], F16)
        tile_tok = sb("tile_tok", [P, TILES, TILES], F16)
        order = sb("order", [P, TILES], I32)
        bound = sb("bound", [P, E - 1], F32)
        past = sb("past", [P, STEPS], F32)
        past2 = sb("past2", [P, STEPS], F32)
        e_of = sb("e_of", [P, STEPS], F32)
        pos = sb("pos", [P, STEPS], F32)
        cnt = sb("cnt", [P, STEPS], F32)
        cnt2 = sb("cnt2", [P, STEPS], F32)
        cnt3 = sb("cnt3", [P, STEPS], F32)
        mask = sb("mask", [P, STEPS], F32)
        last_f = sb("last_f", [P, 1], F32)
        walk_last = sb("walk_last", [P, 1], I32)
        tile_of = sb("tile_of", [P, STEPS], F32)
        walk_f = sb("walk_f", [P, STEPS], F32)
        walk = sb("walk", [P, STEPS], I32)
        gx = sb("gx", [P, 1], F32)
        gf = sb("gf", [P, 1], F32)
        tgx = sb("tgx", [P, 1], F32)
        tgf = sb("tgf", [P, 1], F32)
        tgx24 = sb("tgx24", [P, 1], F32)
        gs_rows = sb("gs_rows", [IC, P], F32)
        us_rows = sb("us_rows", [IC, P], F32)
        gs = sb("gs", [P, IC], F32)
        us = sb("us", [P, IC], F32)
        dsc = sb("dsc", [P, D], F32)
        dsb = sb("dsb", [P, D], F32)
        part_ssq = sb("part_ssq", [P, E], F32)
        m_sum = sb("m_sum", [P, E], F32)
        half_exp = sb("half_exp", [P, E], I32)
        m_exp = sb("m_exp", [P, E], I32)
        m_scale = sb("m_scale", [P, E], F32)
        m_inv = sb("m_inv", [P, E], F32)
        m_inv2 = sb("m_inv2", [P, E], F32)
        z_scale = sb("z_scale", [P, E], F32)
        h_scale = sb("h_scale", [P, E], F32)
        y_scale = sb("y_scale", [P, E], F32)
        stats = sb("stats", [P, 4, 2, 6], F32)
        mv = sb("mv", [P, 4, 2, 2], F32)
        prep = sb("prep", [P, 4, 2, 2], F32)
        ln_tab = sb("ln_tab", [P, ROUNDS, 2, 2], F32)
        step_ln = sb("step_ln", [P, STEPS, 2], F32)
        col_ssq = sb("col_ssq", [P, 2, IC], F32)
        late_norms = sb("late_norms", [P, 2 * KC * KC], F32)
        gu = sb("gu", [P, IC], F32)
        gu2 = sb("gu2", [P, IC], F32)
        nn = sb("nn", [P, IC], F32)
        b2 = sb("b2", [P, IC], F32)
        b2c = sb("b2c", [P, IC], F32)
        b_inv = sb("b_inv", [P, IC], F32)
        f_top = sb("f_top", [P, IC], F32)
        f_scale = sb("f_scale", [P, IC], F32)
        f_inv = sb("f_inv", [P, IC], F32)
        gate_mul = sb("gate_mul", [P, IC], F32)
        up_mul0 = sb("up_mul0", [P, IC], F32)
        up_mul = sb("up_mul", [P, IC], F32)

        bank = [stack.enter_context(nc.psum_tensor(f"bank{i}", [P, 512], F32)) for i in range(8)]
        Z, HT, XT, Y, X2T, SMALL = bank[0], bank[1], bank[2], bank[3], bank[4], bank[6]
        MT_SECOND = [bank[4], bank[3], bank[5], bank[7]]
        MT_NEXT = [bank[5], bank[7], bank[4]]
        MT_FIRST = [bank[5], bank[7], bank[0], bank[1]]
        ACC = [bank[0], bank[1], bank[2], bank[3]]
        GATE = [bank[5], bank[7]]
        UP = [bank[6], bank[4]]

        M_SUM = 192

        consts = sem("consts")
        ids_in = sem("ids_in")
        params_in = sem("params_in")
        ctx_in = [sem("ctx_in0"), sem("ctx_in1")]
        w_in = [sem(f"w_in{i}") for i in range(4)]
        sort_v = sem("sort_v")
        onehot_done = sem("onehot_done")
        counts_done = sem("counts_done")
        rank_read = sem("rank_read")
        place_done = sem("place_done")
        row_hot_done = sem("row_hot_done")
        tile_eq_done = sem("tile_eq_done")
        tile_tok_done = sem("tile_tok_done")
        order_mm = sem("order_mm")
        order_done = sem("order_done")
        gathered = [sem(f"gathered{i}") for i in range(5)]
        mask_done = sem("mask_done")
        walk_done = sem("walk_done")
        scales_T = sem("scales_T")
        scales_done = sem("scales_done")
        tanh_done = sem("tanh_done")
        gates_done = sem("gates_done")
        ssq_done = sem("ssq_done")
        msum_done = sem("msum_done")
        mchain = sem("mchain")
        mscale_done = sem("mscale_done")
        mT_done = sem("mT_done")
        mhi_done = sem("mhi_done")
        mlo_done = sem("mlo_done")
        stats_done = sem("stats_done")
        aggregated = sem("aggregated")
        mv_done = sem("mv_done")
        ln_chain = sem("ln_chain")
        ln_done = sem("ln_done")
        step_ln_done = sem("step_ln_done")
        xn_done = sem("xn_done")
        xT_done = sem("xT_done")
        xhi_done = sem("xhi_done")
        xlo_done = sem("xlo_done")
        z_done = sem("z_done")
        silu_done = sem("silu_done")
        h_done = sem("h_done")
        hT_done = sem("hT_done")
        hhi_done = sem("hhi_done")
        hlo_done = sem("hlo_done")
        y_done = sem("y_done")
        x1_done = sem("x1_done")
        x2n_done = sem("x2n_done")
        x2T_done = sem("x2T_done")
        x2hi_done = sem("x2hi_done")
        x2lo_done = sem("x2lo_done")
        abs_done = sem("abs_done")
        big_done = sem("big_done")
        sum_done = sem("sum_done")
        q_done = sem("q_done")
        sq_done = sem("sq_done")
        scaled = sem("scaled")
        norm_read = sem("norm_read")
        norm_done = sem("norm_done")
        fchain = sem("fchain")
        norms_read = sem("norms_read")
        b2_done = sem("b2_done")
        pool_f = sem("pool_f")
        binv_done = sem("binv_done")
        fscale_done = sem("fscale_done")
        gate_done = sem("gate_done")
        up_done = sem("up_done")
        sg_done = sem("sg_done")
        fuse_done = sem("fuse_done")
        fh_done = sem("fh_done")
        fl_done = sem("fl_done")
        down_done = sem("down_done")
        acc_done = sem("acc_done")
        acc_free = sem("acc_free")
        added = sem("added")
        added_last = sem("added_last")
        stored = sem("stored")

        N_CONSTS = 14

        def slab_tile(g, t):
            v = X2[:, g, :, :, :, :] if isinstance(g, int) else X2[:, ds(g, 1), :, :, :, :]
            pat = "p a k t i -> p (a k t i)" if isinstance(g, int) else "p g a k t i -> p (g a k t i)"
            return v.rearrange(pat).bitcast(F32)[:, t * D:(t + 1) * D]

        def x2_part(tile, part):
            if isinstance(tile, int):
                return X2[:, tile // TPG, part, :, tile % TPG, :]
            return X2[:, ds(tile >> 2, 1), part, :, ds(tile & 3, 1), :].rearrange("p a k b i -> p (a k b) i")

        def x2_group(g, part, k):
            if isinstance(g, int):
                return X2[:, g, part, k, :, :].rearrange("p t i -> p (t i)")
            return X2[:, ds(g, 1), part, k, :, :].rearrange("p g t i -> p (g t i)")

        def slab_slot(n):
            return n % 2 if n < EARLY else n % 4

        def slab_turn(n):
            return sum(slab_slot(m) == slab_slot(n) for m in range(n + 1))

        def slab_before(n):
            return max((m for m in range(n) if slab_slot(m) == slab_slot(n)), default=None)

        def gu_slab(a, k):
            return 2 * KC * a + k if 2 * KC * a + k < EARLY_NORMS else MORE_GU + k - 2

        def down_slab(c):
            return EARLY_NORMS + c if c < 2 * KC else LAST_DOWN + c - 2 * KC

        def experts(s, lo, code):
            if lo % 2 == 0:
                return code & 3, (code >> 2) & 3
            return (s - ((code >> 4) & 15)) & 3, code & 3

        def quantised(lo):
            return 0 if lo < 3 or lo >= STEPS else 1 if 6 <= lo < 12 or 14 <= lo < 18 else 2

        def first_slab(lo):
            return sum(quantised(i) for i in range(lo))

        def slabs_of(s, lo):
            return [s - lo + first_slab(lo) + i for i in range(quantised(lo))]

        def squared_of(s, lo):
            n = 2 if lo in (4, 5) else quantised(lo) if 6 <= lo < STEPS - 1 else 0
            return [s - lo + max(first_slab(lo) - 2, 0) + i for i in range(n)]

        def xs_tile(tile):
            if isinstance(tile, int):
                return xs[:, tile, :]
            return xs[:, ds(tile, 1), :].rearrange("p a d -> p (a d)")

        def ln_col(r, which, i):
            if isinstance(r, int):
                return ln_tab[:, r, which, i:i + 1]
            return ln_tab[:, ds(r, 1), which, i:i + 1].rearrange("p a i -> p (a i)")

        block = stack.enter_context(nc.Block())

        @block.sync
        def _(sp):
            sp.dma_start(ids[:], ids_v).then_inc(ids_in, 16)
            sp.dma_start(cs[:, 0], ctx_v[E - 1]).then_inc(ctx_in[0], 16)
            sp.dma_start(gx[:], g_xattn.partition_broadcast(P)).then_inc(params_in, 16)
            sp.dma_start(gf[:], g_ffn.partition_broadcast(P)).then_inc(params_in, 16)
            sp.dma_start(gs_rows[:], gate_scale.rearrange("(c p) -> c p", p=P)).then_inc(params_in, 16)
            sp.dma_start(us_rows[:], up_scale.rearrange("(c p) -> c p", p=P)).then_inc(params_in, 16)
            sp.dma_start(dsc[:], down_scale.partition_broadcast(P)).then_inc(params_in, 16)
            sp.dma_start(cs[:, 1], ctx_v[E - 2]).then_inc(ctx_in[1], 16)

            def load_slab(n):
                if slab_before(n) is not None:
                    sp.wait_ge(sum_done, slab_before(n) + 1)
                for a in range(3):
                    for k in range(2 * KC):
                        if n == gu_slab(a, k):
                            src = (gate_v if k < KC else up_v)[:, k % KC, a * 512:(a + 1) * 512]
                for c in range(IC):
                    if n == down_slab(c):
                        src = down_v[:, c, :]
                sp.dma_start(ws[:, slab_slot(n)], src).then_inc(w_in[slab_slot(n)], 16)

            load_slab(0)
            load_slab(1)
            for e in range(2, E):
                sp.wait_ge(mT_done, KC * (e - 1))
                sp.wait_ge(ssq_done, e - 1)
                sp.dma_start(cs[:, e % 2], ctx_v[E - 1 - e]).then_inc(ctx_in[e % 2], 16)
            for n in range(2, SLABS):
                load_slab(n)

        @block.gpsimd
        def _(pool):
            g = nc.gpsimd
            g.memset(zero[:], 0.0).then_inc(consts, 1)
            g.memset(ones[:], 1.0).then_inc(consts, 1)
            g.memset(ones32[:], 1.0).then_inc(consts, 1)
            g.memset(mhalf[:], -0.5).then_inc(consts, 1)
            g.memset(ln_half[:], -0.5).then_inc(consts, 1)
            g.memset(ones64[:], 1.0).then_inc(consts, 1)
            g.iota(iota_q[:], pattern=[[1, P]], base=0, channel_multiplier=0,
                   allow_small_or_imprecise_dtypes=True).then_inc(consts, 1)
            g.iota(tok_no[:], pattern=[[1, TILES]], base=0, channel_multiplier=TILES,
                   allow_small_or_imprecise_dtypes=True).then_inc(consts, 1)
            g.iota(step128[:], pattern=[[P, STEPS]], base=0, channel_multiplier=0,
                   allow_small_or_imprecise_dtypes=True).then_inc(consts, 1)
            g.iota(step_pos[:], pattern=[[P, STEPS]], base=0, channel_multiplier=1,
                   allow_small_or_imprecise_dtypes=True).then_inc(consts, 1)
            g.memset(cge[:, 0], 0.0).then_inc(consts, 1)
            g.memset(cge[:, E], 1.0).then_inc(consts, 1)
            pool.wait_ge(consts, N_CONSTS - 2)
            g.affine_select(out=ident[:], in_=zero[:], compare_op=ALU.not_equal, fill=1.0, base=0,
                            pattern=[[-1, P]], channel_multiplier=1).then_inc(consts, 1)
            g.affine_select(out=below[:], in_=ones[:], compare_op=ALU.is_gt, fill=0.0, base=0,
                            pattern=[[1, P]], channel_multiplier=-1).then_inc(consts, 1)

            pool.wait_ge(tile_eq_done, 1)
            g.tensor_tensor(tile_tok[:], tile_eq[:], tok_no[:].unsqueeze(2).to_broadcast([P, TILES, TILES]),
                            ALU.mult).then_inc(tile_tok_done, 1)

            pool.wait_ge(order_done, 1)

            def gather(t, done):
                g.indirect_dma_start(out=xs[:, t, :], out_offset=None, in_=x_rows[:],
                                     in_offset=bass.IndirectOffsetOnAxis(ap=order[:, t:t + 1], axis=0)
                                     ).then_inc(done, 16)

            def ln_scalars(batch, r, slot, nr, lo, hi):
                rr = slice(r, r + nr) if isinstance(r, int) else ds(r, nr)
                sl = slice(slot, slot + nr)
                pool.wait_ge(mv_done, batch + 1)
                g.tensor_tensor(ln_tab[:, rr, lo:hi, 0], prep[:, sl, lo:hi, 1], ln_half[:, 0:nr, lo:hi],
                                ALU.pow).then_inc(ln_chain, 1)
                pool.wait_ge(ln_chain, batch + 1)
                g.tensor_tensor(ln_tab[:, rr, lo:hi, 1], prep[:, sl, lo:hi, 0], ln_tab[:, rr, lo:hi, 0],
                                ALU.mult).then_inc(ln_done, 1)

            def step_scalars(s, tile):
                g.tensor_tensor(step_ln[:, ds(s, 1), :], ln_tab[:, ds(tile, 1), 0, :],
                                mask[:, ds(s, 1)].unsqueeze(2).to_broadcast([P, 1, 2]),
                                ALU.mult).then_inc(step_ln_done, 1)

            for t in range(3):
                gather(t, gathered[min(t, 1)])
            ln_scalars(0, 0, 0, 1, 0, 1)
            pool.wait_ge(ln_done, 1)
            pool.wait_ge(mask_done, 1)
            step_scalars(0, 0)
            gather(3, gathered[1])
            for t in range(4, 7):
                gather(t, gathered[2])
            ln_scalars(1, 1, 1, 1, 0, 1)
            pool.wait_ge(ln_done, 2)
            pool.wait_ge(walk_done, 1)
            tile1 = g.value_load(walk[0:1, 0:1], min_val=0, max_val=4095)
            step_scalars(1, (tile1 >> 4) & 15)
            ln_scalars(2, 2, 2, 2, 0, 1)
            pool.wait_ge(ln_done, 3)
            late_gathers = [[7, 8, 9], [10, 11, 12], [13, 14, 15]]

            def round_slab(n, slot):
                pool.wait_ge(big_done, n + 1)
                if not (isinstance(n, int) and n == 0):
                    pool.wait_ge(q_done, n)
                g.tensor_tensor(w_sum[:], ws[:, slot], w_big[:, slot], ALU.add).then_inc(sum_done, 1)
                pool.wait_ge(sum_done, n + 1)
                dst = W8[:, n, :] if isinstance(n, int) else W8[:, ds(n, 1), :].rearrange("p a n -> p (a n)")
                g.tensor_tensor(dst, w_sum[:], w_big[:, slot], ALU.subtract).then_inc(q_done, 1)

            def ffn_norm(i, lo, hi):
                pool.wait_ge(b2_done, i + 1)
                g.tensor_tensor(b_inv[:, lo:hi], b2c[:, lo:hi], mhalf[:, lo:hi], ALU.pow).then_inc(pool_f, 1)
                pool.wait_ge(pool_f, i + 1)
                g.tensor_scalar(f_top[:, lo:hi], b_inv[:, lo:hi], 2.0 ** 15 / 512, None,
                                ALU.mult).then_inc(binv_done, 1)

            def step(s, lo):
                if lo < STEPS - 2:
                    code = g.value_load(walk[0:1, ds(s + 1, 1)], min_val=0, max_val=4095)
                    if lo >= 2:
                        pool.wait_ge(ln_done, s + 2)
                    step_scalars(s + 2, (code >> 4) & 15)
                ln_scalars(s + BATCH_LEAD, s + STATS1_LEAD, lo % 2, 1, 0 if lo + STATS1_LEAD < TILES else 1,
                           2 if lo >= STATS2_LAG else 1)
                if lo < len(late_gathers):
                    for t in late_gathers[lo]:
                        gather(t, gathered[3 if t < 10 else 4])
                slabs = slabs_of(s, lo)
                for i, n in enumerate(slabs):
                    if lo < STEPS - 1 or i == 0:
                        round_slab(n, (first_slab(lo) + i) % 2)

            for s in range(6):
                step(s, s)
            with pool.Fori(3, 6) as half:
                step(2 * half, 6)
                step(2 * half + 1, 7)
            for s in range(12, STEPS):
                step(s, s)
            ffn_norm(0, 0, 2 * KC)
            ln_scalars(STEPS + BATCH_LEAD, STEPS + STATS1_LEAD, 1, 1, 1, 2)
            for n in range(EARLY - 1, SLABS):
                if n == EARLY + 1:
                    ln_scalars(STEPS + BATCH_LEAD + 1, STEPS + STATS1_LEAD + 1, 0, 1, 1, 2)
                if n == LAST_DOWN + 2:
                    ffn_norm(1, 2 * KC, IC)
                round_slab(n, slab_slot(n))

            for t in range(TILES):
                if t < TILES - TPG:
                    pool.wait_ge(acc_free, TPG + t + 1)
                    g.tensor_tensor(xs[:, t, :], xs[:, t, :], slab_tile(t // TPG, t % TPG),
                                    ALU.add).then_inc(added, 1)
                    pool.wait_ge(added, t + 1)
                else:
                    pool.wait_ge(added_last, t - (TILES - TPG) + 1)
                g.indirect_dma_start(out=out_rows[:], out_offset=bass.IndirectOffsetOnAxis(
                    ap=order[:, t:t + 1], axis=0), in_=xs[:, t, :], in_offset=None).then_inc(stored, 16)
            pool.wait_ge(stored, 16 * TILES)

        @block.scalar
        def _(act):
            a = nc.scalar
            def squares(e):
                act.wait_ge(ctx_in[e % 2], 16 * (e // 2 + 1))
                if e:
                    act.wait_ge(ssq_done, e)
                a.activation(junk[:], cs[:, e % 2].rearrange("p r d -> p (r d)"), ACT.Square,
                             accum_out=part_ssq[:, e:e + 1]).then_inc(ssq_done, 1)

            def expert_high(e, chunks, banks):
                act.wait_ge(mscale_done, e + 1)
                for k in chunks:
                    act.wait_ge(mT_done, KC * e + k + 1)
                    a.activation(Mh[:, (e * KC + k) * 512:(e * KC + k + 1) * 512], banks[k % len(banks)][:],
                                 ACT.Identity, scale=m_scale[:, e:e + 1]).then_inc(mhi_done, 1)

            def normalise(s, tile):
                act.wait_ge(step_ln_done, s + 1)
                if isinstance(s, int):
                    mul, add = step_ln[:, s, 0:1], step_ln[:, s, 1:2]
                else:
                    mul, add = (step_ln[:, ds(s, 1), i:i + 1].rearrange("p a i -> p (a i)") for i in range(2))
                a.activation(xn[:], xs_tile(tile), ACT.Identity, scale=mul, bias=add).then_inc(xn_done, 1)

            def x_high(s):
                act.wait_ge(xT_done, s + 1)
                a.activation(xTh[:], XT[:], ACT.Copy, scale=X_SCALE).then_inc(xhi_done, 1)

            def normalise2(tile):
                act.wait_ge(ln_done, tile + STATS2_LAG + BATCH_LEAD + 1)
                if not (isinstance(tile, int) and tile == 0):
                    act.wait_ge(x2T_done, tile)
                r = tile + STATS1_LEAD + STATS2_LAG
                a.activation(x2n[:], xs_tile(tile), ACT.Identity, scale=ln_col(r, 1, 0),
                             bias=ln_col(r, 1, 1)).then_inc(x2n_done, 1)

            def x2_high(tile, src):
                act.wait_ge(x2T_done, tile + 1)
                a.activation(x2_part(tile, 0), src[:].rearrange("p (k i) -> p k i", k=KC),
                             ACT.Copy, scale=X_SCALE).then_inc(x2hi_done, 1)

            def slab_abs(n, slot, count, before):
                act.wait_ge(w_in[slot], 16 * count)
                if before is not None:
                    act.wait_ge(q_done, before + 1)
                a.activation(w_big[:, slot], ws[:, slot], ACT.Abs, scale=FP8_STEP).then_inc(abs_done, 1)

            def slab_square(n, slot, count):
                act.wait_ge(q_done, n + 1)
                if not (isinstance(count, int) and count < 2):
                    act.wait_ge(norm_done, count - 1)
                w = W8[:, n, :] if isinstance(n, int) else W8[:, ds(n, 1), :].rearrange("p a n -> p (a n)")
                a.activation(sq[:, slot, :], w, ACT.Square).then_inc(sq_done, 1)

            def scale_down(c):
                act.wait_ge(fscale_done, 1 + c // (2 * KC))
                act.wait_ge(q_done, down_slab(c) + 1)
                w = W8[:, down_slab(c), :]
                a.activation(w, w, ACT.Copy, scale=f_inv[:, c:c + 1]).then_inc(scaled, 1)

            squares(0)
            act.wait_ge(params_in, 80)
            a.activation(tgx[:], gx[:], ACT.Tanh).then_inc(tanh_done, 1)
            a.activation(tgf[:], gf[:], ACT.Tanh).then_inc(tanh_done, 1)
            a.activation(warm[:], gx[:], ACT.Silu)
            expert_high(0, range(KC), MT_FIRST)
            squares(1)
            normalise(0, 0)
            x_high(0)
            squares(2)
            act.wait_ge(walk_done, 1)

            def step(s, lo):
                prev, nxt = lo >= 1, lo < STEPS - 1
                code = a.value_load(walk[0:1, ds(s, 1)], min_val=0, max_val=4095)
                e = code & 3
                if prev:
                    act.wait_ge(hT_done, s)
                    if lo >= 2:
                        act.wait_ge(y_done, s - 1)
                    a.activation(hTh[:], HT[:], ACT.Copy).then_inc(hhi_done, 1)
                if nxt:
                    act.wait_ge(xT_done, s + 1)
                    if lo >= 2:
                        act.wait_ge(x1_done, s - 1)
                    if lo == 0:
                        act.wait_ge(gathered[1], 48)
                    normalise(s + 1, (code >> 4) & 15)
                for i, n in enumerate(slabs_of(s, lo)):
                    slot = (first_slab(lo) + i) % 2
                    if isinstance(n, int):
                        slab_abs(n, slot, slab_turn(n), slab_before(n))
                    else:
                        slab_abs(n, slot, (n - slot + 2) >> 1, n - 2)
                if lo == 0:
                    expert_high(1, range(KC), MT_SECOND)
                elif lo + 1 < E:
                    expert_high(lo + 1, range(KC - 1), MT_NEXT)
                act.wait_ge(z_done, s + 1)
                if prev:
                    act.wait_ge(h_done, s)
                a.activation(silu_z[:], Z[:], ACT.Silu, scale=z_scale[:, ds(e, 1)]).then_inc(silu_done, 1)
                if nxt:
                    x_high(s + 1)
                if 1 <= lo < E - 1:
                    expert_high(lo + 1, [KC - 1], MT_NEXT)
                if lo >= X2_LAG:
                    x2_high(s - X2_LAG, X2T)
                for i, n in enumerate(squared_of(s, lo)):
                    slab_square(n, (max(first_slab(lo) - 2, 0) + i) % 2, n)
                if lo + 1 >= X2_LAG:
                    normalise2(s + 1 - X2_LAG)
                if lo == 0:
                    squares(3)

            for s in range(6):
                step(s, s)
            with act.Fori(3, 6) as half:
                step(2 * half, 6)
                step(2 * half + 1, 7)
            step(12, 12)
            step(13, 13)
            with act.Fori(7, 9) as half:
                step(2 * half, 14)
                step(2 * half + 1, 15)
            step(STEPS - 1, STEPS - 1)

            def last_h_high():
                act.wait_ge(hT_done, STEPS)
                act.wait_ge(y_done, STEPS - 1)
                a.activation(hTh[:], HT[:], ACT.Copy).then_inc(hhi_done, 1)

            def gate_silu(g, c):
                act.wait_ge(gate_done, g * IC + c + 1)
                if isinstance(g, int) and g == 0 and c % (2 * KC) == 0:
                    act.wait_ge(fscale_done, 1 + c // (2 * KC))
                if not (isinstance(g, int) and g * IC + c < 2):
                    act.wait_ge(fuse_done, g * IC + c - 1)
                a.activation(sg[:, c % 2, :], GATE[c % 2][:], ACT.Silu,
                             scale=gate_mul[:, c:c + 1]).then_inc(sg_done, 1)

            def fuse_high(g, c):
                act.wait_ge(fuse_done, g * IC + c + 1)
                if not (isinstance(g, int) and g * IC + c < 2):
                    act.wait_ge(down_done, g * IC + c - 1)
                a.activation(fh[:, c % 2, :], fuse[:, c % 2, :], ACT.Copy).then_inc(fh_done, 1)

            def late_abs(c):
                for n in range(EARLY + 2 * c, min(EARLY + 2 * c + 2, SLABS)):
                    slab_abs(n, slab_slot(n), slab_turn(n), slab_before(n))

            def late_second(c):
                for i in range(2):
                    if 4 <= c < 7:
                        n = MORE_GU + 2 * (c - 4) + i
                        slab_square(n, i, EARLY_NORMS + n - MORE_GU)
                    if 2 <= c < 4:
                        scale_down(KC + 2 * (c - 2) + i)
                    if 7 <= c < 9:
                        scale_down(2 * KC + 2 * (c - 7) + i)

            last_h_high()
            late_abs(0)
            x2_high(TILES - 3, XT)
            gate_silu(0, 0)
            normalise2(TILES - 2)
            scale_down(0)
            fuse_high(0, 0)
            x2_high(TILES - 2, XT)
            normalise2(TILES - 1)
            scale_down(1)
            gate_silu(0, 1)
            x2_high(TILES - 1, XT)
            fuse_high(0, 1)
            late_abs(1)
            scale_down(2)
            scale_down(3)

            def group(g, first, last):
                for c in range(2, IC):
                    gate_silu(g, c)
                    if first:
                        late_abs(c)
                    fuse_high(g, c)
                    if first:
                        late_second(c)
                if not last:
                    for c in range(2):
                        gate_silu(g + 1, c)
                        fuse_high(g + 1, c)

            group(0, True, False)
            with act.Fori(1, GROUPS - 1) as gi:
                group(gi, False, False)
            group(GROUPS - 1, False, True)

        @block.vector
        def _(dve):
            v = nc.vector
            chained = [0]

            def link(ins, s_, count):
                count[0] += 1
                ins.then_inc(s_, 1)
                dve.wait_ge(s_, count[0])

            mcount = [0]

            def expert_scale(e, between=None):
                c = slice(e, e + 1)
                dve.wait_ge(msum_done, e + 1)
                src = X2T[:, 0:1] if e == 0 else SMALL[:, M_SUM + e:M_SUM + e + 1]
                link(v.tensor_scalar(m_sum[:, c], src, 2.0 ** -40, 2.0 ** 80,
                                     ALU.max, ALU.min), mchain, mcount)
                link(v.tensor_scalar(half_exp[:, c], m_sum[:, c].bitcast(I32), 24, None,
                                     ALU.arith_shift_right), mchain, mcount)
                link(v.tensor_scalar(m_exp[:, c], half_exp[:, c], -1.0, float(127 + 77), ALU.mult, ALU.add),
                     mchain, mcount)
                if between is not None:
                    between()
                link(v.tensor_scalar(m_scale[:, c].bitcast(I32), m_exp[:, c], 23, None,
                                     ALU.logical_shift_left), mchain, mcount)
                link(v.reciprocal(m_inv[:, c], m_scale[:, c]), mchain, mcount)
                v.tensor_scalar(z_scale[:, c], m_inv[:, c], 1.0 / X_SCALE, None, ALU.mult)
                v.tensor_scalar(h_scale[:, c], m_scale[:, c], 2.0 ** -24 / X_SCALE, None, ALU.mult)
                v.tensor_tensor(m_inv2[:, c], m_inv[:, c], m_inv[:, c], ALU.mult).then_inc(mscale_done, 1)

            def expert_y_scale(e):
                c = slice(e, e + 1)
                dve.wait_ge(mscale_done, e + 1)
                v.scalar_tensor_tensor(out=y_scale[:, c], in0=m_inv2[:, c], scalar=tgx24[:, 0:1], in1=m_inv[:, c],
                                       op0=ALU.mult, op1=ALU.mult)

            def prepare(slot0, slot1, lo, hi):
                sl = slice(slot0, slot1)
                v.tensor_scalar(prep[:, sl, lo:hi, 0], mv[:, sl, lo:hi, 0], -1.0, None, ALU.mult)
                v.tensor_scalar(prep[:, sl, lo:hi, 1], mv[:, sl, lo:hi, 1], LN_EPS, None, ALU.add).then_inc(mv_done, 1)

            dve.wait_ge(ids_in, 16)
            dve.wait_ge(consts, N_CONSTS)
            for j in range(1, E):
                ins = v.tensor_scalar(cge[:, j], ids[:], float((E - j) * PER_EXPERT), None, ALU.is_ge)
            link(ins, sort_v, chained)
            v.tensor_tensor(onehot[:], cge[:, 1:E + 1, :].rearrange("p e c -> p (e c)"),
                            cge[:, 0:E, :].rearrange("p e c -> p (e c)"), ALU.subtract).then_inc(onehot_done, 1)
            dve.wait_ge(counts_done, 1)
            total = SMALL[:, 64:128]
            link(v.tensor_tensor_scan(incl[:], ones64[:], total, 0.0, ALU.mult, ALU.add), sort_v, chained)
            link(v.tensor_tensor(base[:], incl[:], total, ALU.subtract), sort_v, chained)
            v.tensor_tensor(rank_e[:], SMALL[:, 0:64], base[:], ALU.add).then_inc(rank_read, 1)
            dve.wait_ge(rank_read, 1)
            link(v.tensor_tensor(rank_m[:], rank_e[:], onehot[:], ALU.mult), sort_v, chained)
            link(v.tensor_reduce(rank_f[:], rank_m[:].rearrange("p (e c) -> p c e", e=E), AX.X, ALU.add),
                 sort_v, chained)
            link(v.tensor_copy(rank_i[:], rank_f[:]), sort_v, chained)
            v.tensor_scalar(tile_i[:], rank_i[:], 7, None, ALU.arith_shift_right)
            link(v.tensor_scalar(row_i[:], rank_i[:], P - 1, None, ALU.bitwise_and), sort_v, chained)
            v.tensor_copy(row_f[:], row_i[:])
            v.tensor_copy(tile_f[:], tile_i[:]).then_inc(place_done, 1)
            dve.wait_ge(place_done, 1)
            v.tensor_tensor(tile_eq[:], iota_q[:, 0:TILES].unsqueeze(1).to_broadcast([P, TILES, TILES]),
                            tile_f[:].unsqueeze(2).to_broadcast([P, TILES, TILES]),
                            ALU.is_equal).then_inc(tile_eq_done, 1)
            for c in range(TILES):
                ins = v.tensor_scalar(row_hot[:, c, :], iota_q[:], row_f[:, c:c + 1], None, ALU.is_equal)
                if c % 4 == 3:
                    ins.then_inc(row_hot_done, 1)

            def copy_order():
                dve.wait_ge(order_mm, 1)
                v.tensor_copy(order[:], SMALL[:, 128:128 + TILES]).then_inc(order_done, 1)

            expert_scale(0, copy_order)

            starts = [base[:, e * TILES:e * TILES + 1] for e in range(1, E)]
            for e in range(1, E):
                ins = v.tensor_scalar(bound[:, e - 1:e], starts[e - 1], float(TOK - 1), float(P * e - P),
                                      ALU.min, ALU.add)
            link(ins, sort_v, chained)
            link(v.tensor_scalar(past[:], step128[:], bound[:, 0:1], None, ALU.is_gt), sort_v, chained)
            link(v.scalar_tensor_tensor(out=past2[:], in0=step128[:], scalar=bound[:, 1:2], in1=past[:],
                                        op0=ALU.is_gt, op1=ALU.add), sort_v, chained)
            link(v.scalar_tensor_tensor(out=e_of[:], in0=step128[:], scalar=bound[:, 2:3], in1=past2[:],
                                        op0=ALU.is_gt, op1=ALU.add), sort_v, chained)
            v.scalar_tensor_tensor(out=pos[:], in0=e_of[:], scalar=-float(P), in1=step_pos[:],
                                   op0=ALU.mult, op1=ALU.add).then_inc(sort_v, 1)
            chained[0] += 1
            dve.wait_ge(sort_v, chained[0])
            v.tensor_scalar(cnt[:], pos[:], starts[0], None, ALU.is_ge).then_inc(sort_v, 1)
            dve.wait_ge(gathered[0], 16)
            v.bn_stats(stats[:, 0, 0, :], xs[:, 0, :]).then_inc(stats_done, 1)
            chained[0] += 1
            dve.wait_ge(sort_v, chained[0])
            v.scalar_tensor_tensor(out=cnt2[:], in0=pos[:], scalar=starts[1], in1=cnt[:],
                                   op0=ALU.is_ge, op1=ALU.add).then_inc(sort_v, 1)
            chained[0] += 1
            dve.wait_ge(stats_done, 1)
            v.bn_aggr(mv[:, 0, 0, :], stats[:, 0, 0, :]).then_inc(aggregated, 1)
            dve.wait_ge(sort_v, chained[0])
            v.scalar_tensor_tensor(out=cnt3[:], in0=pos[:], scalar=starts[2], in1=cnt2[:],
                                   op0=ALU.is_ge, op1=ALU.add).then_inc(sort_v, 1)
            chained[0] += 1
            dve.wait_ge(aggregated, 1)
            prepare(0, 1, 0, 1)
            dve.wait_ge(sort_v, chained[0])
            v.tensor_tensor(mask[:], cnt3[:], e_of[:], ALU.is_equal).then_inc(mask_done, 1)

            dve.wait_ge(scales_T, 1)
            v.tensor_copy(gs[:], SMALL[:, 160:160 + IC])
            v.tensor_copy(us[:], SMALL[:, 176:176 + IC]).then_inc(scales_done, 1)

            def expert_low(e, chunks, banks):
                dve.wait_ge(mscale_done, e + 1)
                for k in chunks:
                    w = slice((e * KC + k) * 512, (e * KC + k + 1) * 512)
                    dve.wait_ge(mhi_done, KC * e + k + 1)
                    v.scalar_tensor_tensor(out=Ml[:, w], in0=banks[k % len(banks)][:], scalar=m_scale[:, e:e + 1],
                                           in1=Mh[:, w], op0=ALU.mult, op1=ALU.subtract).then_inc(mlo_done, 1)

            def slab_big(n, slot):
                dve.wait_ge(abs_done, n + 1)
                v.tensor_scalar(w_big[:, slot], w_big[:, slot], FP8_FLOOR, None, ALU.max).then_inc(big_done, 1)

            def tile_stats(slot, which, tile):
                return v.bn_stats(stats[:, slot, which, :], xs_tile(tile))

            def aggregate(batch, slots, lo, hi):
                dve.wait_ge(stats_done, batch + 1)
                if not (isinstance(batch, int) and batch < BATCH_LEAD):
                    dve.wait_ge(ln_done, batch - 1)
                dve.nop(nofuse=True)
                for slot in slots:
                    for i in range(lo, hi):
                        ins = v.bn_aggr(mv[:, slot, i, :], stats[:, slot, i, :])
                ins.then_inc(aggregated, 1)
                dve.wait_ge(aggregated, batch + 1)
                dve.nop(nofuse=True)
                prepare(slots[0], slots[-1] + 1, lo, hi)

            def x_low(dst, src, high, ready, n):
                dve.wait_ge(ready, n)
                return v.scalar_tensor_tensor(out=dst, in0=src, scalar=X_SCALE, in1=high, op0=ALU.mult,
                                              op1=ALU.subtract)

            def x2_low(tile, src):
                return x_low(x2_part(tile, 1), src[:].rearrange("p (k i) -> p k i", k=KC), x2_part(tile, 0),
                             x2hi_done, tile + 1)

            def h_low(s, lo):
                dve.wait_ge(hhi_done, s + 1)
                if lo >= 1:
                    dve.wait_ge(y_done, s)
                v.tensor_tensor(hTl[:], HT[:], hTh[:], ALU.subtract).then_inc(hlo_done, 1)

            expert_low(0, range(2), MT_FIRST)
            dve.wait_ge(mask_done, 1)
            v.tensor_copy(walk_f[:], e_of[:])
            link(v.scalar_tensor_tensor(out=tile_of[:], in0=step128[:], scalar=1.0 / P, in1=e_of[:],
                                        op0=ALU.mult, op1=ALU.subtract), sort_v, chained)
            link(v.scalar_tensor_tensor(out=walk_f[:, 1:], in0=e_of[:, :-1], scalar=4.0, in1=walk_f[:, 1:],
                                        op0=ALU.mult, op1=ALU.add), sort_v, chained)
            link(v.scalar_tensor_tensor(out=walk_f[:, :-1], in0=tile_of[:, 1:], scalar=16.0, in1=walk_f[:, :-1],
                                        op0=ALU.mult, op1=ALU.add), sort_v, chained)
            link(v.scalar_tensor_tensor(out=walk_f[:, 1:], in0=tile_of[:, :-1], scalar=256.0, in1=walk_f[:, 1:],
                                        op0=ALU.mult, op1=ALU.add), sort_v, chained)
            v.tensor_scalar(last_f[:], tile_of[:, STEPS - 1:STEPS], 64.0, e_of[:, STEPS - 1:STEPS], ALU.mult, ALU.add)
            link(v.tensor_copy(walk[:], walk_f[:]), sort_v, chained)
            v.tensor_scalar(walk_last[:], last_f[:], 4.0, None, ALU.mult).then_inc(walk_done, 1)

            expert_low(0, range(2, KC), MT_FIRST)
            x_low(xTl[:], XT[:], xTh[:], xhi_done, 1).then_inc(xlo_done, 1)
            dve.wait_ge(gathered[1], 48)
            tile_stats(1, 0, 1).then_inc(stats_done, 1)
            aggregate(1, [1], 0, 1)
            expert_scale(1)
            tile_stats(2, 0, 2)
            tile_stats(3, 0, 3).then_inc(stats_done, 1)
            aggregate(2, [2, 3], 0, 1)

            dve.wait_ge(tanh_done, 2)
            v.tensor_scalar(tgx24[:], tgx[:], 2.0 ** 24, None, ALU.mult).then_inc(gates_done, 1)
            v.tensor_scalar(dsb[:], dsc[:], tgf[:, 0:1], None, ALU.mult).then_inc(gates_done, 1)
            dve.wait_ge(gates_done, 2)
            expert_y_scale(0)


            def add_expert(s, e, tile, xn_reads):
                dve.wait_ge(y_done, s + 1)
                if xn_reads is not None:
                    dve.wait_ge(xn_done, xn_reads)
                row = xs_tile(tile)
                v.scalar_tensor_tensor(out=row, in0=Y[:], scalar=y_scale[:, ds(e, 1)], in1=row,
                                       op0=ALU.mult, op1=ALU.add).then_inc(x1_done, 1)

            fcount, nread = [0], [0]

            def ffn_norms(norms, a0, a1):
                if a0 == 0:
                    dve.wait_ge(scales_done, 1)
                    dve.wait_ge(norm_done, EARLY_NORMS)
                    v.tensor_copy(late_norms[:, 0:2 * KC], SMALL[:, 4 * KC * KC:4 * KC * KC + 2 * KC])
                for a in range(a0, a1):
                    src = norms[:, (a - a0) * 2 * KC * KC:(a - a0 + 1) * 2 * KC * KC]
                    ins = v.tensor_reduce(col_ssq[:, :, a * KC:(a + 1) * KC],
                                          src.rearrange("p (w k j) -> p w j k", w=2, k=KC), AX.X, ALU.add)
                link(ins, norms_read, nread)
                c = slice(a0 * KC, a1 * KC)
                v.tensor_tensor(nn[:, c], col_ssq[:, 0, c], col_ssq[:, 1, c], ALU.mult)
                link(v.tensor_tensor(gu[:, c], gs[:, c], us[:, c], ALU.mult), fchain, fcount)
                link(v.tensor_tensor(gu2[:, c], gu[:, c], gu[:, c], ALU.mult), fchain, fcount)
                link(v.tensor_tensor(b2[:, c], nn[:, c], gu2[:, c], ALU.mult), fchain, fcount)
                v.tensor_scalar(b2c[:, c], b2[:, c], 1e-30, 1e38, ALU.max, ALU.min).then_inc(b2_done, 1)

            def ffn_scales(i, a0, a1):
                c = slice(a0 * KC, a1 * KC)
                dve.wait_ge(binv_done, i + 1)
                link(v.tensor_scalar(f_scale[:, c].bitcast(I32), f_top[:, c].bitcast(I32), POW2_MASK, None,
                                     ALU.bitwise_and), fchain, fcount)
                v.tensor_scalar(gate_mul[:, c], gs[:, c], 1.0 / X_SCALE, None, ALU.mult)
                link(v.tensor_scalar(up_mul0[:, c], us[:, c], 1.0 / X_SCALE, None, ALU.mult), fchain, fcount)
                v.tensor_tensor(up_mul[:, c], up_mul0[:, c], f_scale[:, c], ALU.mult)
                v.reciprocal(f_inv[:, c], f_scale[:, c]).then_inc(fscale_done, 1)

            def step(s, lo, code):
                prev, nxt = lo >= 1, lo < STEPS - 1
                e, e_prev = experts(s, lo, code)
                tile_prev = (code >> 8) & 15 if lo % 2 == 0 else (s - 1 - e_prev) & 15
                if prev:
                    h_low(s - 1, lo - 1)
                if lo == 0:
                    dve.wait_ge(gathered[2], 48)
                if lo == 3:
                    dve.wait_ge(gathered[3], 48)
                if lo == 6:
                    dve.wait_ge(gathered[4], 96)
                first, last = (0 if lo + STATS1_LEAD < TILES else 1), (2 if lo >= STATS2_LAG else 1)
                slot = lo % 2
                if first == 0:
                    ins = tile_stats(slot, 0, s + STATS1_LEAD)
                if last == 2:
                    dve.wait_ge(x1_done, s - 1)
                    ins = tile_stats(slot, 1, s - STATS2_LAG)
                ins.then_inc(stats_done, 1)
                aggregate(s + BATCH_LEAD, [slot], first, last)
                for i, n in enumerate(slabs_of(s, lo)):
                    slab_big(n, (first_slab(lo) + i) % 2)
                if lo + 1 < E:
                    expert_y_scale(lo + 1)
                    expert_low(lo + 1, range(KC - 1), MT_NEXT if lo else MT_SECOND)
                dve.wait_ge(silu_done, s + 1)
                if prev:
                    dve.wait_ge(hT_done, s)
                v.scalar_tensor_tensor(out=h[:], in0=Z[:], scalar=h_scale[:, ds(e, 1)], in1=silu_z[:],
                                       op0=ALU.mult, op1=ALU.mult).then_inc(h_done, 1)
                if nxt:
                    x_low(xTl[:], XT[:], xTh[:], xhi_done, s + 2).then_inc(xlo_done, 1)
                if lo + 1 < E:
                    expert_low(lo + 1, [KC - 1], MT_NEXT if lo else MT_SECOND)
                if lo >= X2_LAG:
                    x2_low(s - X2_LAG, X2T).then_inc(x2lo_done, 1)
                if lo == STEPS - 1:
                    ffn_norms(SMALL, 0, 2)
                if prev:
                    add_expert(s - 1, e_prev, tile_prev, s + 2 if nxt else None)
                if lo + 2 < E:
                    expert_scale(lo + 2)

            def two_steps(half, lo):
                code = v.value_load(walk[0:1, ds(2 * half, 1)], min_val=0, max_val=4095)
                step(2 * half, lo, code)
                if lo < STEPS - 1:
                    step(2 * half + 1, lo + 1, code)

            for half in range(3):
                two_steps(half, 2 * half)
            with dve.Fori(3, 6) as half:
                two_steps(half, 6)
            two_steps(6, 12)
            with dve.Fori(7, 9) as half:
                two_steps(half, 14)
            two_steps(STEPS // 2, STEPS - 1)

            last = v.value_load(walk_last[0:1, 0:1], min_val=0, max_val=4095)
            h_low(STEPS - 1, STEPS - 1)
            dve.wait_ge(x1_done, STEPS - 1)
            tile_stats(1, 1, TILES - 2).then_inc(stats_done, 1)
            aggregate(STEPS + BATCH_LEAD, [1], 1, 2)
            ffn_scales(0, 0, 2)

            def late_slabs(c):
                for n in range(EARLY + 2 * c, min(EARLY + 2 * c + 2, SLABS)):
                    slab_big(n, slab_slot(n))

            def late_norm(c):
                dve.wait_ge(norm_done, EARLY_NORMS + 2 * (c - 4))
                v.tensor_copy(late_norms[:, 2 * KC * (c - 4):2 * KC * (c - 3)],
                              GATE[(c + 1) % 2][:, 0:2 * KC]).then_inc(norm_read, 1)

            def unit_fuse(g, c):
                u = g * IC + c
                dve.wait_ge(up_done, u + 1)
                dve.wait_ge(sg_done, u + 1)
                if not (isinstance(g, int) and g * IC + c < 2):
                    dve.wait_ge(fl_done, u - 1)
                v.scalar_tensor_tensor(out=fuse[:, c % 2, :], in0=UP[c % 2][:], scalar=up_mul[:, c:c + 1],
                                       in1=sg[:, c % 2, :], op0=ALU.mult, op1=ALU.mult).then_inc(fuse_done, 1)

            def unit_low(g, c):
                u = g * IC + c
                if not (isinstance(g, int) and g * IC + c < 2):
                    dve.wait_ge(down_done, u - 1)
                dve.wait_ge(fh_done, u + 1)
                v.tensor_tensor(fl[:, c % 2, :], fuse[:, c % 2, :], fh[:, c % 2, :],
                                ALU.subtract).then_inc(fl_done, 1)

            x2_low(TILES - 3, XT).then_inc(x2lo_done, 1)
            late_slabs(0)
            unit_fuse(0, 0)
            add_expert(STEPS - 1, (last >> 2) & 3, (last >> 8) & 15, None)
            dve.wait_ge(x1_done, STEPS)
            tile_stats(0, 1, TILES - 1).then_inc(stats_done, 1)
            aggregate(STEPS + BATCH_LEAD + 1, [0], 1, 2)
            unit_low(0, 0)
            x2_low(TILES - 2, XT).then_inc(x2lo_done, 1)
            unit_fuse(0, 1)
            x2_low(TILES - 1, XT).then_inc(acc_free, TPG)
            unit_low(0, 1)
            late_slabs(1)

            def group(g, first, last):
                for c in range(2, IC):
                    unit_fuse(g, c)
                    if first and 5 <= c < 8:
                        late_norm(c)
                    unit_low(g, c)
                    if first:
                        late_slabs(c)
                    if first and c == 7:
                        dve.wait_ge(norm_read, 3)
                        ffn_norms(late_norms, 2, 3)
                        ffn_scales(1, 2, 3)
                if not last:
                    unit_fuse(g + 1, 0)
                    unit_low(g + 1, 0)
                for t in range(TPG):
                    if t < TPG - 1:
                        dve.wait_ge(acc_done, g * (TPG - 1) + t + 1)
                    else:
                        dve.wait_ge(down_done, g * IC + IC)
                    v.tensor_tensor(slab_tile(g, t), ACC[t][:], dsb[:], ALU.mult).then_inc(acc_free, 1)
                    if last:
                        dve.wait_ge(acc_free, TPG + g * TPG + t + 1)
                        v.tensor_tensor(xs[:, g * TPG + t, :], xs[:, g * TPG + t, :], slab_tile(g, t),
                                        ALU.add).then_inc(added_last, 1)
                if not last:
                    unit_fuse(g + 1, 1)
                    unit_low(g + 1, 1)

            group(0, True, False)
            with dve.Fori(1, GROUPS - 1) as gi:
                group(gi, False, False)
            group(GROUPS - 1, False, True)

        @block.tensor
        def _(pe):
            t_ = nc.tensor

            def transpose4(dst, src, done):
                for k in range(KC):
                    ins = t_.matmul(dst[:, k * P:(k + 1) * P], src[:, k * P:(k + 1) * P], ident[:],
                                    is_transpose=True, start=(k == 0), stop=(k == KC - 1))
                ins.then_inc(done, 1)

            pe.wait_ge(consts, N_CONSTS)
            pe.wait_ge(onehot_done, 1)
            t_.matmul(SMALL[:, 0:64], below[:], onehot[:], start=True, stop=True)
            t_.matmul(SMALL[:, 64:128], ones[:], onehot[:], start=True, stop=True).then_inc(counts_done, 1)

            def expert_turn(e, chunks, banks):
                pe.wait_ge(ctx_in[e % 2], 16 * (e // 2 + 1))
                for k in chunks:
                    if e == 1 and k == 0:
                        pe.wait_ge(mscale_done, 1)
                    if e == 1 and k >= 2:
                        pe.wait_ge(mlo_done, k - 1)
                    if e >= 2 and k == 0:
                        pe.wait_ge(mlo_done, KC * e)
                    if e >= 2 and k == KC - 1:
                        pe.wait_ge(mlo_done, KC * e + 1)
                    for r in range(KC):
                        ins = t_.matmul(banks[k % len(banks)][:, r * P:(r + 1) * P], cs[:, e % 2, r, k * P:(k + 1) * P],
                                        ident[:], is_transpose=True, start=(r == 0), stop=(r == KC - 1))
                    ins.then_inc(mT_done, 1)

            def expert_sum(e):
                pe.wait_ge(ssq_done, e + 1)
                if e == 1:
                    pe.wait_ge(scales_done, 1)
                if e >= 1:
                    pe.wait_ge(mscale_done, e)
                dst = X2T[:, 0:1] if e == 0 else SMALL[:, M_SUM + e:M_SUM + e + 1]
                t_.matmul(dst, ones32[:], part_ssq[:, e:e + 1], start=True,
                          stop=True).then_inc(msum_done, 1)

            expert_turn(0, range(KC - 1), MT_FIRST)
            expert_sum(0)
            pe.wait_ge(tile_tok_done, 1)
            pe.wait_ge(rank_read, 1)
            for c in range(TILES):
                if c % 4 == 0:
                    pe.wait_ge(row_hot_done, c // 4 + 1)
                ins = t_.matmul(SMALL[:, 128:128 + TILES], row_hot[:, c, :], tile_tok[:, c, :],
                                start=(c == 0), stop=(c == TILES - 1))
            ins.then_inc(order_mm, 1)
            pe.wait_ge(params_in, 80)
            pe.wait_ge(order_done, 1)
            t_.matmul(SMALL[:, 160:160 + IC], gs_rows[:], ident[0:IC, 0:IC], is_transpose=True, start=True, stop=True)
            t_.matmul(SMALL[:, 176:176 + IC], us_rows[:], ident[0:IC, 0:IC], is_transpose=True, start=True,
                      stop=True).then_inc(scales_T, 1)
            expert_turn(0, [KC - 1], MT_FIRST)
            expert_turn(1, range(KC), MT_SECOND)
            expert_sum(1)
            pe.wait_ge(xn_done, 1)
            transpose4(XT, xn, xT_done)
            pe.wait_ge(walk_done, 1)

            def product(dst, e, high, low, done):
                n = 0
                for k in range(KC):
                    mh = Mh[:, ds(e * (KC * 512) + k * 512, 512)]
                    ml = Ml[:, ds(e * (KC * 512) + k * 512, 512)]
                    for lhs, rhs in ((high, mh), (high, ml), (low, mh)):
                        ins = t_.matmul(dst[:], lhs[:, k * P:(k + 1) * P], rhs, start=(n == 0), stop=(n == 3 * KC - 1))
                        n += 1
                ins.then_inc(done, 1)

            def turn_h(s):
                pe.wait_ge(h_done, s + 1)
                transpose4(HT, h, hT_done)

            def turn_x2(tile, dst):
                pe.wait_ge(x2n_done, tile + 1)
                if not (isinstance(tile, int) and tile == 0):
                    pe.wait_ge(x2lo_done, tile)
                transpose4(dst, x2n, x2T_done)

            def product_y(s, e):
                pe.wait_ge(hlo_done, s + 1)
                if not (isinstance(s, int) and s == 0):
                    pe.wait_ge(x1_done, s)
                product(Y, e, hTh, hTl, y_done)

            def step(s, lo, code):
                e, e_prev = experts(s, lo, code)
                if lo >= 1:
                    if lo >= 2:
                        pe.wait_ge(hlo_done, s - 1)
                    turn_h(s - 1)
                if 1 <= lo < E - 1:
                    expert_turn(lo + 1, range(KC - 1), MT_NEXT)
                pe.wait_ge(xlo_done, s + 1)
                pe.wait_ge(mlo_done, KC * (min(lo, E - 1) + 1))
                product(Z, e, xTh, xTl, z_done)
                if lo < STEPS - 1:
                    pe.wait_ge(xn_done, s + 2)
                    transpose4(XT, xn, xT_done)
                if 1 <= lo < E - 1:
                    expert_turn(lo + 1, [KC - 1], MT_NEXT)
                if lo >= X2_LAG:
                    turn_x2(s - X2_LAG, X2T)
                if lo >= 1:
                    product_y(s - 1, e_prev)
                for i, n in enumerate(squared_of(s, lo)):
                    norms(n, n, (max(first_slab(lo) - 2, 0) + i) % 2, SMALL, KC * n)
                if lo + 2 < E:
                    expert_sum(lo + 2)

            def norms(n, count, slot, dst, col):
                pe.wait_ge(sq_done, count + 1)
                if isinstance(n, int) and n == 0:
                    pe.wait_ge(mscale_done, E)
                for j in range(KC):
                    out_col = dst[:, col + j:col + j + 1] if isinstance(col, int) else dst[:, ds(col + j, 1)]
                    ins = t_.matmul(out_col, sq[:, slot, j * P:(j + 1) * P], ones[:, 0:1], start=True, stop=True)
                ins.then_inc(norm_done, 1)

            def two_steps(half, lo):
                code = t_.value_load(walk[0:1, ds(2 * half, 1)], min_val=0, max_val=4095)
                step(2 * half, lo, code)
                if lo < STEPS - 1:
                    step(2 * half + 1, lo + 1, code)

            for half in range(3):
                two_steps(half, 2 * half)
            with pe.Fori(3, 6) as half:
                two_steps(half, 6)
            two_steps(6, 12)
            with pe.Fori(7, 9) as half:
                two_steps(half, 14)
            two_steps(STEPS // 2, STEPS - 1)

            def late_norms_of(c):
                pe.wait_ge(sg_done, c)
                for i in range(2):
                    norms(MORE_GU + 2 * (c - 5) + i, EARLY_NORMS + 2 * (c - 5) + i, i, GATE[(c + 1) % 2], i * KC)

            def gate_up(g, c):
                a, j = c // KC, c % KC
                if isinstance(g, int) and g == 0 and 6 <= c < 9:
                    pe.wait_ge(norm_read, c - 5)
                for dst, first, free, done in ((GATE, 0, sg_done, gate_done), (UP, KC, fuse_done, up_done)):
                    if not (isinstance(g, int) and g * IC + c < 2):
                        pe.wait_ge(free, g * IC + c - 1)
                    for k in range(KC):
                        w = W8[:, gu_slab(a, first + k), j * P:(j + 1) * P]
                        for part in range(2):
                            ins = t_.matmul(dst[c % 2][:], w, x2_group(g, part, k), start=(k == 0 and part == 0),
                                            stop=(k == KC - 1 and part == 1))
                    ins.then_inc(done, 1)

            def down(g, c):
                pe.wait_ge(fl_done, g * IC + c + 1)
                if isinstance(g, int) and g == 0:
                    pe.wait_ge(scaled, c + 1)
                for t in range(TPG):
                    if c == 0:
                        pe.wait_ge(acc_free, g * TPG + t + 1)
                    for part in (fh, fl):
                        ins = t_.matmul(ACC[t][:], part[:, c % 2, t * P:(t + 1) * P], W8[:, down_slab(c), :],
                                        start=(c == 0 and part is fh), stop=(c == IC - 1 and part is fl))
                    if c == IC - 1 and t < TPG - 1:
                        ins.then_inc(acc_done, 1)
                ins.then_inc(down_done, 1)

            code = t_.value_load(walk_last[0:1, 0:1], min_val=0, max_val=4095)
            pe.wait_ge(hlo_done, STEPS - 1)
            turn_h(STEPS - 1)
            pe.wait_ge(xlo_done, STEPS)
            turn_x2(TILES - 3, XT)
            pe.wait_ge(norms_read, 1)
            gate_up(0, 0)
            product_y(STEPS - 1, (code >> 2) & 3)
            turn_x2(TILES - 2, XT)
            gate_up(0, 1)
            turn_x2(TILES - 1, XT)
            gate_up(0, 2)
            down(0, 0)
            down(0, 1)

            def group(g, first, last):
                for c in range(3 if first else 2, IC):
                    gate_up(g, c)
                    if first and 5 <= c < 8:
                        late_norms_of(c)
                    down(g, c - 1)
                if not last:
                    gate_up(g + 1, 0)
                down(g, IC - 1)
                if not last:
                    gate_up(g + 1, 1)
                    down(g + 1, 0)

            group(0, True, False)
            with pe.Fori(1, GROUPS - 1) as gi:
                group(gi, False, False)
            group(GROUPS - 1, False, True)


_INS = ["x", "itok_BxS_13_99985", "ctx_2048", "g_xattn", "g_ffn", "L0_ffn_gate_w", "L0_ffn_up_w", "L0_ffn_down_w",
        "L0_ffn_gate_scale", "L0_ffn_up_scale", "L0_ffn_down_scale"]


def kernel(**inputs):
    import numpy as np
    import concourse.bacc as bacc
    from concourse.bass_utils import run_bass_kernel_spmd as run

    nc = bacc.Bacc("TRN2", target_bir_lowering=False, num_devices=1)
    arrays, args = {}, []
    for name in _INS:
        a = np.ascontiguousarray(inputs[name])
        arrays["in_" + name] = a
        args.append(nc.dram_tensor("in_" + name, a.shape, mybir.dt.from_np(a.dtype), kind="ExternalInput").ap())
    args.append(nc.dram_tensor("out_0", inputs["x"].shape, mybir.dt.float32, kind="ExternalOutput").ap())
    build(nc, *args)
    r = run(nc, [arrays], core_ids=[0])
    return r.results[0]["out_0"]
```
